# Optimizing a Trainium2 kernel written in Bass

```python
import numpy as np
import jax
import jax.numpy as jnp

def _softmax(x, axis=-1):
    return jax.nn.softmax(x, axis=axis)

def _gelu(x):
    return jax.nn.gelu(x, approximate=True)

def _silu(x):
    return jax.nn.silu(x)

def _sigmoid(x):
    return jax.nn.sigmoid(x)

def _layernorm(x, axis=-1, eps=1e-05):
    m = jnp.mean(x, axis=axis, keepdims=True)
    v = jnp.var(x, axis=axis, keepdims=True)
    return (x - m) / jnp.sqrt(v + eps)

def _scatter_add(tgt, idx, src, axis=0):
    return tgt.at[idx].add(src)

def _segment_sum(src, seg, n):
    return jax.ops.segment_sum(src, seg, n)
kernel_name = 'mk_adaln_d1_jaxref_r8_d32ec3'

def setup_inputs(seed: int=0):
    np.random.seed(seed)
    _w = jnp.asarray

    def _L0_attn_setup():
        import jax, jax.numpy as jnp
        import numpy as np
        DIM = 128
        NUM_HEADS = 16
        DIM_HEAD = 64
        INNER = NUM_HEADS * DIM_HEAD

        def rotate_half(t):
            x1, x2 = jnp.split(t, 2, axis=-1)
            return jnp.concatenate([-x2, x1], axis=-1)

        def rope_pos(n, d, dtype=jnp.float32):
            inv_freq = 1.0 / 10000.0 ** (jnp.arange(0, d, 2, dtype=jnp.float32) / d)
            freqs = jnp.arange(n, dtype=jnp.float32)[:, None] * inv_freq[None, :]
            return jnp.concatenate([freqs, freqs], axis=-1).astype(dtype)

        def apply_rope(pos, t):
            return t * jnp.cos(pos) + rotate_half(t) * jnp.sin(pos)
        key = jax.random.key(seed)
        k1, k2, k3, k4 = jax.random.split(key, 4)
        b, n = (2, 256)
        x = jax.random.normal(k1, (b, n, DIM), dtype=jnp.float32)
        s = DIM ** (-0.5)
        Wq = jax.random.normal(k2, (DIM, INNER), dtype=jnp.float32) * s
        Wkv = jax.random.normal(k3, (DIM, 2 * DIM_HEAD), dtype=jnp.float32) * s
        Wo = jax.random.normal(k4, (INNER, DIM), dtype=jnp.float32) * INNER ** (-0.5)
        return {'x': x, 'Wq': Wq, 'Wkv': Wkv, 'Wo': Wo}
    _L0_attn_in = _L0_attn_setup()

    def _L0_ffn_setup():
        import jax, jax.numpy as jnp
        import numpy as np
        TOP_K = 2
        N_EXPERTS = 8
        key = jax.random.key(seed)
        k1, k2, k3, k4 = jax.random.split(key, 4)
        B, C, L, O, E = (8, 512, 128, 128, N_EXPERTS)
        scale = 1.0 / np.sqrt(L)
        return {'x': jax.random.normal(k1, (B, C, L), dtype=jnp.float32), 'gate_w': jax.random.normal(k2, (E, L), dtype=jnp.float32) * scale, 'expert_w': jax.random.normal(k3, (E, O, L), dtype=jnp.float32) * scale, 'expert_b': jax.random.normal(k4, (E, O), dtype=jnp.float32) * scale}
    _L0_ffn_in = _L0_ffn_setup()
    _L0_c = _w((lambda *s: np.random.randn(*s).astype(np.float32) * 0.05)(2, 128))
    _L0_wmod = _w((lambda *s: np.random.randn(*s).astype(np.float32) * 0.05)(128, 6 * 128) * 128 ** (-0.5))
    _d = {'L0_attn_x': _L0_attn_in['x'], 'L0_attn_Wq': _L0_attn_in['Wq'], 'L0_attn_Wkv': _L0_attn_in['Wkv'], 'L0_attn_Wo': _L0_attn_in['Wo'], 'L0_ffn_gate_w': _L0_ffn_in['gate_w'], 'L0_ffn_expert_w': _L0_ffn_in['expert_w'], 'L0_ffn_expert_b': _L0_ffn_in['expert_b'], 'L0_c': _L0_c, 'L0_wmod': _L0_wmod}
    _x0 = _d['L0_attn_x']
    _d['L0_attn_x'] = jax.random.normal(jax.random.fold_in(jax.random.key(seed), 1), (2, 1024, 128), dtype=_x0.dtype)
    del _x0
    return _d

def reference(L0_attn_x, L0_attn_Wq, L0_attn_Wkv, L0_attn_Wo, L0_ffn_gate_w, L0_ffn_expert_w, L0_ffn_expert_b, L0_c, L0_wmod):

    def _L0_attn_ref(x, Wq, Wkv, Wo):
        import jax, jax.numpy as jnp
        import numpy as np
        DIM = 128
        NUM_HEADS = 16
        DIM_HEAD = 64
        INNER = NUM_HEADS * DIM_HEAD

        def rotate_half(t):
            x1, x2 = jnp.split(t, 2, axis=-1)
            return jnp.concatenate([-x2, x1], axis=-1)

        def rope_pos(n, d, dtype=jnp.float32):
            inv_freq = 1.0 / 10000.0 ** (jnp.arange(0, d, 2, dtype=jnp.float32) / d)
            freqs = jnp.arange(n, dtype=jnp.float32)[:, None] * inv_freq[None, :]
            return jnp.concatenate([freqs, freqs], axis=-1).astype(dtype)

        def apply_rope(pos, t):
            return t * jnp.cos(pos) + rotate_half(t) * jnp.sin(pos)
        b, n, _ = x.shape
        scale = DIM_HEAD ** (-0.5)
        q = x @ Wq
        kv = x @ Wkv
        k, v = jnp.split(kv, 2, axis=-1)
        q = q.reshape(b, n, NUM_HEADS, DIM_HEAD).transpose(0, 2, 1, 3)
        pos = rope_pos(n, DIM_HEAD, x.dtype)
        q = apply_rope(pos, q)
        k = apply_rope(pos, k)
        q = q * scale
        sim = jnp.einsum('bhid,bjd->bhij', q, k)
        causal = jnp.triu(jnp.ones((n, n), dtype=bool), k=1)
        neg = -jnp.finfo(sim.dtype).max
        sim = jnp.where(causal, neg, sim)
        sim = sim - jnp.max(sim, axis=-1, keepdims=True)
        attn = jax.nn.softmax(sim, axis=-1)
        out = jnp.einsum('bhij,bjd->bhid', attn, v)
        out = out.transpose(0, 2, 1, 3).reshape(b, n, INNER)
        return out @ Wo

    def _L0_ffn_ref(x, gate_w, expert_w, expert_b):
        import jax, jax.numpy as jnp
        import numpy as np
        TOP_K = 2
        N_EXPERTS = 8
        B, C, L = x.shape
        E, O, _ = expert_w.shape
        xt = x.reshape(-1, L)
        router_logits = jnp.einsum('tl,el->te', xt, gate_w)
        probs = jax.nn.softmax(router_logits.astype(jnp.float32), axis=-1)
        routing_weights, selected = jax.lax.top_k(probs, TOP_K)
        comb = jnp.sum(jax.nn.one_hot(selected, E, dtype=routing_weights.dtype) * routing_weights[..., None], axis=1)
        comb = comb.astype(x.dtype)
        out = jnp.zeros((xt.shape[0], O), dtype=x.dtype)
        for e in range(E):
            ye = xt @ expert_w[e].T + expert_b[e]
            out = out + ye * comb[:, e:e + 1]
        return out.reshape(B, C, O)
    x = L0_attn_x
    mod = (_silu(L0_c) @ L0_wmod).reshape(L0_c.shape[0], 6, 1, -1)
    sa, ca, ga, sb, cb, gb = (mod[:, 0], mod[:, 1], mod[:, 2], mod[:, 3], mod[:, 4], mod[:, 5])
    ga = (2 * (ga >= 0) - 1) * jnp.maximum(jnp.abs(ga), 0.25)
    gb = (2 * (gb >= 0) - 1) * jnp.maximum(jnp.abs(gb), 0.25)
    h = _layernorm(x, axis=-1) * (1 + ca) + sa
    x = x + ga * _L0_attn_ref(h, L0_attn_Wq, L0_attn_Wkv, L0_attn_Wo)
    h = _layernorm(x, axis=-1) * (1 + cb) + sb
    x = x + gb * _L0_ffn_ref(h, L0_ffn_gate_w, L0_ffn_expert_w, L0_ffn_expert_b)
    return x

_drawn_inputs = setup_inputs


def setup_inputs(seed=0):
    import zlib

    import numpy as np

    out = dict(_drawn_inputs(seed))
    spreads = {}
    factors = {'L0_ffn_expert_b': 6.066}
    for name, (base, spread) in spreads.items():
        noise = np.random.default_rng([zlib.crc32(name.encode()), seed]).standard_normal(out[name].shape)
        drawn = base * np.exp(spread * noise) if base else spread * noise
        out[name] = jnp.asarray(drawn.astype(out[name].dtype))
    for name, factor in factors.items():
        out[name] = (out[name] * factor).astype(out[name].dtype)
    return out
```

```python
import numpy as np
import concourse.bass as bass
from concourse import mybir
from contextlib import ExitStack


B, N, DIM = 2, 1024, 128
HEADS, DH = 16, 64
HALF = DH // 2
EXPERTS, TOPK = 8, 2
T = 128
TILES = N // T
PAIRS = HEADS // 2
STEPS = PAIRS * B
TOTAL = TILES * STEPS
BANK = 512
SCALE = float(DH) ** -0.5
EPS = 1e-5
MASKED = 3.0e38
SA, CA, GA, SB, CB, GB = range(6)

LOOP_FROM, LOOP_TO = 4, 14
SLOTS = (0, 1, 2, 3, 14, 15)


def blocks(j):
    return j + 1


def uses(j):
    return 1 if blocks(j) <= 4 else 2


def stages(j, step):
    table = {
        0: [("norm1_T", j + 1)],
        1: [("kv", j + 1), ("q0", j + 1), ("norm2_T", j - 2)],
        2: [("q1", j + 1), ("router", j - 2)],
        3: [("k_T", j + 1), ("comb_T", j - 2)],
        14: [("recip_T", j - 1), ("ffn0", j - 2)],
        15: [("wo", j - 1), ("ffn1", j - 2)],
    }
    return [(name, t) for name, t in table.get(step, []) if 0 <= t < TILES]


TAIL = [("norm2_T", TILES - 2), ("recip_T", TILES - 1), ("router", TILES - 2), ("wo", TILES - 1),
        ("comb_T", TILES - 2), ("norm2_T", TILES - 1), ("ffn0", TILES - 2), ("router", TILES - 1),
        ("ffn1", TILES - 2), ("comb_T", TILES - 1), ("ffn0", TILES - 1), ("ffn1", TILES - 1)]
FILLS = {"norm1_T": (1, 0), "kv": (0, 1), "q0": (1, 1), "q1": (1, 1), "k_T": (1, 0),
         "recip_T": (2, 2), "wo": (1, 0), "norm2_T": (0, 1), "router": (1, 0), "comb_T": (0, 1),
         "ffn0": (2, 1), "ffn1": (2, 1)}
HEAD = [("norm1_T", 0), ("kv", 0), ("q0", 0), ("q1", 0), ("k_T", 0)]


def ledger():
    a, b = 1, 1
    at_step, at_stage = {}, {}

    def stage(name, t):
        nonlocal a, b
        at_stage[name, t] = (a, b)
        a, b = a + FILLS[name][0], b + FILLS[name][1]

    for name, t in HEAD:
        stage(name, t)
    for j in range(TILES):
        for step in range(STEPS):
            at_step[j, step] = (a, b)
            a, b = a + uses(j), b + uses(j)
            for name, t in stages(j, step):
                stage(name, t)
    for name, t in TAIL:
        stage(name, t)
    return at_step, at_stage


AT_STEP, AT_STAGE = ledger()

RSTD = {(1, 0): 1, (1, 1): 2}
for _j in range(TILES):
    if _j >= 2:
        RSTD[2, _j - 2] = len(RSTD) + 1
    if _j + 2 < TILES:
        RSTD[1, _j + 2] = len(RSTD) + 1
for _j in (TILES - 2, TILES - 1):
    RSTD[2, _j] = len(RSTD) + 1


def bank_counts(j, step):
    if isinstance(step, int):
        return AT_STEP[j, step]
    a, b = AT_STEP[j, LOOP_FROM]
    return (step - LOOP_FROM) * uses(j) + a, (step - LOOP_FROM) * uses(j) + b


def build(nc, x, wq, wkv, wo, gate, expert_w, expert_b, c_t, wmod,
          cos_q, sin_q, cos_k, sin_k, ident, mask, out):
    f32, f32r, bf16, u32 = mybir.dt.float32, mybir.dt.float32r, mybir.dt.bfloat16, mybir.dt.uint32
    ALU, ACT, AX = mybir.AluOpType, mybir.ActivationFunctionType, mybir.AxisListType

    ctx = ExitStack()
    with ctx:
        def sb(name, shape, dt=f32):
            return ctx.enter_context(nc.sbuf_tensor(name, shape, dt))

        def bank(name, shape):
            return ctx.enter_context(nc.psum_tensor(name, shape, f32))

        def sem(name):
            return ctx.enter_context(nc.semaphore(name))

        x_sb = sb("x_sb", [T, B, TILES, DIM])
        wq_sb = sb("wq_sb", [DIM, HEADS * DH])
        wkv_sb = sb("wkv_sb", [DIM, 2 * DH])
        wo_sb = sb("wo_sb", [2 * DH, PAIRS, DIM])
        we_sb = sb("we_sb", [DIM, EXPERTS * DIM])
        gate_sb = sb("gate_sb", [DIM, EXPERTS])
        eb_sb = sb("eb_sb", [EXPERTS, DIM])
        wmod_sb = sb("wmod_sb", [DIM, 6 * DIM])
        c_sb = sb("c_sb", [DIM, B])
        cosq_sb, sinq_sb, cosk_sb, sink_sb = (sb(n, [T, TILES, DH]) for n in ("cosq", "sinq", "cosk", "sink"))
        ident_sb = sb("ident_sb", [T, T])
        mask_sb = sb("mask_sb", [T, T])
        ident_bf = sb("ident_bf", [T, T], bf16)
        mask_bf = sb("mask_bf", [T, T], bf16)
        minus_half = sb("minus_half", [T, B])
        iota_sb = sb("iota_sb", [T, EXPERTS])
        silu = sb("silu", [DIM, 3, B])
        silu_rows = sb("silu_rows", [DIM, B, T])
        mod_cols = sb("mod_cols", [DIM, 4, B])
        gates = sb("gates", [T, 2, B, DIM])
        gate_tmp = sb("gate_tmp", [T, 2, 2 * B * DIM])
        stats = sb("stats", [T, B, 6])
        mean_var = sb("mean_var", [T, B, 2])
        var_eps = sb("var_eps", [T, B])
        rstd = sb("rstd", [T, B])
        normed1 = sb("normed1", [T, B, DIM])
        stats2 = sb("stats2", [T, B, 6])
        mean_var2 = sb("mean_var2", [T, B, 2])
        var_eps2 = sb("var_eps2", [T, B])
        rstd2 = sb("rstd2", [T, B])
        normed2 = sb("normed2", [T, B, DIM])
        h1T = sb("h1T", [DIM, B, T])
        h2T = sb("h2T", [DIM, 2, B, T])
        k_split = sb("k_split", [T, B, 3, DH], f32r)
        k_cos = sb("k_cos", [T, B, DH])
        k_sin = sb("k_sin", [T, B, DH])
        k_stack = sb("k_stack", [2 * DH, 2, B, N], f32r)
        v_sb = sb("v_sb", [T, B, TILES, DH])
        rope_cos = sb("rope_cos", [T, 2, 8, DH])
        rope_sin = sb("rope_sin", [T, 2, 8, DH])
        q_split = sb("q_split", [T, 2, B, HEADS, 2, DH], f32r)
        q_feed = [sb(f"q_feed{i}", [T, 2, 2 * DH]) for i in range(2)]
        qT = [sb(f"qT{i}", [2 * DH, 2, T], f32r) for i in range(2)]
        least = sb("least", [T, 2])
        P = [sb(f"P{i}", [T, N]) for i in range(2)]
        PT = [[sb(f"PT{i}{h}", [T, N]) for h in range(2)] for i in range(2)]
        sums = [sb(f"sums{i}", [T, B, HEADS]) for i in range(2)]
        recips = sb("recips", [T, B, HEADS])
        recip_rows = sb("recip_rows", [T, B, HEADS * DH])
        oT = [sb(f"oT{i}", [2 * DH, B, PAIRS, T]) for i in range(2)]
        oT_n = sb("oT_n", [2 * DH, B, PAIRS, T])
        attn = sb("attn", [T, B, DIM])
        logits = sb("logits", [T, B, EXPERTS])
        sorted_l = sb("sorted_l", [T, B, 8])
        neg_top = sb("neg_top", [T, B])
        e_sorted = sb("e_sorted", [T, B, 8])
        e_sum = sb("e_sum", [T, B])
        e_rec = sb("e_rec", [T, B])
        top_idx = sb("top_idx", [T, B, 8], u32)
        top_idx_f = sb("top_idx_f", [T, B, 8])
        top_w = sb("top_w", [T, B, TOPK])
        comb_k = sb("comb_k", [T, B, TOPK, EXPERTS])
        comb = sb("comb", [T, B, EXPERTS])
        combT = sb("combT", [EXPERTS, B, T])
        y = [sb(f"y{b}", [T, 2, DIM]) for b in range(B)]
        out_sb = [sb(f"out_sb{b}", [T, DIM]) for b in range(B)]

        S = [bank(f"S{h}", [T, N]) for h in range(2)]
        bankA = bank("bankA", [T, BANK])
        bankB = bank("bankB", [T, BANK])
        o_ps = bank("o_ps", [T, BANK])
        q_ps = bank("q_ps", [T, BANK])

        loaded = {n: sem(f"loaded_{n}") for n in ("x0", "x1", "mod", "tables", "consts", "w", "late")}
        masks_ready = sem("masks_ready")
        consts_ready = sem("consts_ready")
        silu_exp = sem("silu_exp")
        silu_ready = sem("silu_ready")
        mod_ready = sem("mod_ready")
        stats_ready = sem("stats_ready")
        rstd_ready = sem("rstd_ready")
        normed1_ready = sem("normed1_ready")
        normed2_ready = sem("normed2_ready")
        fullA, fullB = sem("fullA"), sem("fullB")
        freeA, freeB = sem("freeA"), sem("freeB")
        k_parts = sem("k_parts")
        k_ready = sem("k_ready")
        rope_parts = sem("rope_parts")
        rope_sum = sem("rope_sum")
        rope_high = sem("rope_high")
        q_ready = sem("q_ready")
        q_fed = [sem(f"q_fed{i}") for i in range(2)]
        q_turned = sem("q_turned")
        qT_ready = sem("qT_ready")
        scores = [sem("scores_even"), sem("scores_odd")]
        least_ready = [sem("least_even"), sem("least_odd")]
        probs = [sem("probs_even"), sem("probs_odd")]
        pv_done = sem("pv_done")
        o_free = sem("o_free")
        recips_ready = sem("recips_ready")
        rows_ready = sem("rows_ready")
        attn_ready = sem("attn_ready")
        x1_ready = sem("x1_ready")
        sorted_ready = sem("sorted_ready")
        router_exp = sem("router_exp")
        comb_ready = sem("comb_ready")
        y_ready = sem("y_ready")
        out_ready = sem("out_ready")
        stored = sem("stored")
        dve_link, pool_link = sem("dve_link"), sem("pool_link")

        block = ctx.enter_context(nc.Block())

        @block.sync
        def _(sp):
            x_v = x.rearrange("b (j p) d -> p b j d", p=T)
            for b in range(B):
                sp.dma_start(x_sb[:, b, 0:2, :], x_v[:, b, 0:2, :]).then_inc(loaded["x0"], 16)
            sp.dma_start(ident_sb[:], ident).then_inc(loaded["consts"], 16)
            sp.dma_start(wkv_sb[:], wkv).then_inc(loaded["w"], 16)
            sp.dma_start(wq_sb[:], wq).then_inc(loaded["w"], 16)
            sp.dma_start(cosq_sb[:], cos_q.rearrange("(j p) d -> p j d", p=T)).then_inc(loaded["tables"], 16)
            sp.dma_start(sinq_sb[:], sin_q.rearrange("(j p) d -> p j d", p=T)).then_inc(loaded["tables"], 16)
            for b in range(B):
                sp.dma_start(x_sb[:, b, 2:TILES, :], x_v[:, b, 2:TILES, :]).then_inc(loaded["x1"], 16)
            sp.dma_start(wo_sb[:], wo.rearrange("(h p) d -> p h d", p=2 * DH)).then_inc(loaded["late"], 16)
            sp.dma_start(we_sb[:], expert_w).then_inc(loaded["late"], 16)
            sp.dma_start(gate_sb[:], gate).then_inc(loaded["late"], 16)
            sp.dma_start(eb_sb[:], expert_b).then_inc(loaded["late"], 16)

            def feed(j, hp, b, s):
                if not (isinstance(s, int) and s < 2):
                    sp.wait_ge(q_turned, s - 1)
                sp.dma_start(q_feed[b][:].rearrange("p h d -> p (h d)"),
                             q_split[:, j % 2, b].bitcast(f32).rearrange("p h s d -> p (h s d)")
                             [:, bass.ds(hp * 4 * DH, 4 * DH)]).then_inc(q_fed[b], 16)

            def store(t):
                for b in range(B):
                    sp.wait_ge(out_ready, B * t + b + 1)
                    sp.dma_start(out[b, t * T:(t + 1) * T, :], out_sb[b][:]).then_inc(stored, 16)

            for j in range(TILES):
                sp.wait_ge(q_ready, 4 * (j + 1))
                for b in range(B):
                    feed(j, 0, b, j * STEPS + b)
                with sp.Fori(1, PAIRS) as hp:
                    for b in range(B):
                        feed(j, hp, b, hp * 2 + (j * STEPS + b))
                if j >= 3:
                    store(j - 3)
            for t in range(TILES - 3, TILES):
                store(t)
            sp.wait_ge(stored, 16 * B * TILES)

        @block.tensor
        def _(pe):
            def fill(free, count):
                pe.wait_ge(free, count)

            def queries(s, b):
                pe.wait_ge(q_fed[b], s * 8 + (16 - 8 * b))
                if not (isinstance(s, int) and s < 1):
                    pe.wait_ge(qT_ready, s)
                nc.tensor.transpose(q_ps[:, 0:T], q_feed[b][:, 0, :], ident_sb[:])
                nc.tensor.transpose(q_ps[:, T:2 * T], q_feed[b][:, 1, :], ident_sb[:]).then_inc(q_turned, 1)

            def qk(j, s, b, h):
                if h == 0:
                    pe.wait_ge(qT_ready, s + 1)
                if not (isinstance(s, int) and s < 1):
                    pe.wait_ge(probs[h], s)
                width = blocks(j) * T
                for c0 in range(0, width, BANK):
                    c1 = min(c0 + BANK, width)
                    nc.tensor.matmul(S[h][:, c0:c1], qT[b][:, h, :], k_stack[:, 0, b, c0:c1],
                                     start=True, stop=False)
                    last = nc.tensor.matmul(S[h][:, c0:c1], qT[b][:, h, :], k_stack[:, 1, b, c0:c1],
                                            start=False, stop=(c1 < width))
                last = nc.tensor.matmul(S[h][:, width - T:width], ident_bf[:], mask_bf[:],
                                        start=False, stop=True)
                last.then_inc(scores[h], 1)

            def turn_probs(j, s, step, h):
                a, b = bank_counts(j, step)
                pe.wait_ge(probs[h], s + 1)
                nb = blocks(j)
                if uses(j) == 1:
                    chunks = [((bankA, bankB)[h], (fullA, fullB)[h], (freeA, freeB)[h], (a, b)[h], 0, nb)]
                else:
                    chunks = [(bankA, fullA, freeA, a + h, 0, 4), (bankB, fullB, freeB, b + h, 4, nb)]
                for bank_, full, free, count, k0, k1 in chunks:
                    fill(free, count)
                    for k in range(k0, k1):
                        last = nc.tensor.transpose(bank_[:, (k - k0) * T:(k - k0 + 1) * T],
                                                   P[h][:, k * T:(k + 1) * T], ident_sb[:])
                    last.then_inc(full, 1)

            def pv(j, s, step, b):
                a_count, b_count = bank_counts(j, step)
                pe.wait_ge(freeA, a_count + uses(j))
                pe.wait_ge(freeB, b_count + uses(j))
                if not (isinstance(s, int) and s < 1):
                    pe.wait_ge(o_free, s)
                nb = blocks(j)
                for k in range(nb):
                    for h in range(2):
                        last = nc.tensor.matmul(o_ps[h * DH:(h + 1) * DH, 0:T], v_sb[:, b, k, :],
                                                PT[b][h][:, k * T:(k + 1) * T],
                                                start=(k == 0), stop=(k == nb - 1))
                last.then_inc(pv_done, 1)

            def stage(name, t):
                a, b = AT_STAGE[name, t]
                if name == "norm1_T":
                    pe.wait_ge(normed1_ready, t + 1)
                    fill(freeA, a)
                    for i in range(B):
                        last = nc.tensor.transpose(bankA[:, i * T:(i + 1) * T], normed1[:, i, :], ident_sb[:])
                    last.then_inc(fullA, 1)
                elif name == "kv":
                    pe.wait_ge(freeA, a)
                    fill(freeB, b)
                    for i in range(B):
                        last = nc.tensor.matmul(bankB[:, i * 2 * DH:(i + 1) * 2 * DH], h1T[:, i, :], wkv_sb[:],
                                                start=True, stop=True)
                    last.then_inc(fullB, 1)
                elif name in ("q0", "q1"):
                    i = int(name[1])
                    for bank_, full, free, count, c in ((bankA, fullA, freeA, a, 0), (bankB, fullB, freeB, b, 1)):
                        fill(free, count)
                        nc.tensor.matmul(bank_[:], h1T[:, i, :], wq_sb[:, c * BANK:(c + 1) * BANK],
                                         start=True, stop=True).then_inc(full, 1)
                elif name == "k_T":
                    pe.wait_ge(k_ready, t + 1)
                    fill(freeA, a)
                    for k in range(2):
                        for i in range(B):
                            last = nc.tensor.transpose(
                                bankA[:, (2 * k + i) * T:(2 * k + i + 1) * T],
                                k_split[:, i, k:k + 2, :].bitcast(f32).rearrange("p s d -> p (s d)"), ident_sb[:])
                    last.then_inc(fullA, 1)
                elif name == "recip_T":
                    pe.wait_ge(rows_ready, t + 1)
                    for i in range(B):
                        for half, (bank_, full, free, count) in enumerate(
                                ((bankA, fullA, freeA, a + i), (bankB, fullB, freeB, b + i))):
                            fill(free, count)
                            for k in range(4):
                                c = (4 * half + k) * T
                                last = nc.tensor.transpose(bank_[:, k * T:(k + 1) * T],
                                                           recip_rows[:, i, c:c + T], ident_sb[:])
                            last.then_inc(full, 1)
                elif name == "wo":
                    ra, rb = AT_STAGE["recip_T", t]
                    pe.wait_ge(freeA, ra + 2)
                    pe.wait_ge(freeB, rb + 2)
                    fill(freeA, a)
                    for i in range(B):
                        for hp in range(PAIRS):
                            last = nc.tensor.matmul(bankA[:, i * DIM:(i + 1) * DIM], oT_n[:, i, hp, :],
                                                    wo_sb[:, hp, :], start=(hp == 0), stop=(hp == PAIRS - 1))
                    last.then_inc(fullA, 1)
                elif name == "norm2_T":
                    pe.wait_ge(normed2_ready, t + 1)
                    fill(freeB, b)
                    for i in range(B):
                        last = nc.tensor.transpose(bankB[:, i * T:(i + 1) * T], normed2[:, i, :], ident_sb[:])
                    last.then_inc(fullB, 1)
                elif name == "router":
                    nb_ = AT_STAGE["norm2_T", t][1]
                    pe.wait_ge(freeB, nb_ + 1)
                    fill(freeA, a)
                    for i in range(B):
                        last = nc.tensor.matmul(bankA[:, i * EXPERTS:(i + 1) * EXPERTS], h2T[:, t % 2, i, :], gate_sb[:],
                                                start=True, stop=True)
                    last.then_inc(fullA, 1)
                elif name == "comb_T":
                    pe.wait_ge(comb_ready, t + 1)
                    fill(freeB, b)
                    for i in range(B):
                        last = nc.tensor.transpose(bankB[0:EXPERTS, i * T:(i + 1) * T], comb[:, i, :], ident_sb[:])
                    last.then_inc(fullB, 1)
                elif name in ("ffn0", "ffn1"):
                    i = int(name[3])
                    cb = AT_STAGE["comb_T", t][1]
                    pe.wait_ge(freeB, cb + 1)
                    fill(freeA, a)
                    nc.tensor.matmul(bankA[:, 0:DIM], combT[:, i, :], eb_sb[:],
                                     start=True, stop=True).then_inc(fullA, 1)
                    for bank_, full, free, count, c in ((bankB, fullB, freeB, b, 0), (bankA, fullA, freeA, a + 1, 1)):
                        fill(free, count)
                        nc.tensor.matmul(bank_[:], h2T[:, t % 2, i, :], we_sb[:, c * BANK:(c + 1) * BANK],
                                         start=True, stop=True).then_inc(full, 1)

            def one_step(j, step, b, prev, nxt):
                s = step + j * STEPS
                nb2 = b
                if nxt is not None and not (isinstance(s, int) and s + 2 >= TOTAL):
                    queries(s + 2, nb2)
                for h in range(2):
                    if nxt is not None:
                        qk(nxt, s + 1, 1 - b, h)
                    turn_probs(j, s, step, h)
                if prev is not None:
                    pj, pstep = prev
                    pv(pj, s - 1, pstep, 1 - b)

            pe.wait_ge(silu_ready, 1)
            for n, m in enumerate((SA, CA, SB, CB)):
                last = nc.tensor.matmul(bankA[:, n * B:(n + 1) * B], wmod_sb[:, m * DIM:(m + 1) * DIM],
                                        silu[:, 2, :], start=True, stop=True)
            last.then_inc(fullA, 1)
            for n, m in enumerate((GA, GB)):
                for i in range(B):
                    last = nc.tensor.matmul(bankB[:, (n * B + i) * DIM:(n * B + i + 1) * DIM], silu_rows[:, i, :],
                                            wmod_sb[:, m * DIM:(m + 1) * DIM], start=True, stop=True)
            last.then_inc(fullB, 1)
            pe.wait_ge(loaded["consts"], 32)
            pe.wait_ge(loaded["w"], 32)
            for name, t in HEAD:
                stage(name, t)
            queries(0, 0)
            queries(1, 1)
            ka, kb = AT_STAGE["k_T", 0]
            pe.wait_ge(freeA, ka + 1)
            pe.wait_ge(masks_ready, 1)
            for h in range(2):
                qk(0, 0, 0, h)
            for j in range(TILES):
                for step in list(range(LOOP_FROM)) + [None] + list(range(LOOP_TO, STEPS)):
                    if step is None:
                        with pe.Fori(LOOP_FROM // 2, LOOP_TO // 2) as hp:
                            for b in range(B):
                                at = hp * 2 + b
                                one_step(j, at, b, (j, at - 1), j)
                        continue
                    prev = (j, step - 1) if step else ((j - 1, STEPS - 1) if j else None)
                    nxt = j if step < STEPS - 1 else (j + 1 if j + 1 < TILES else None)
                    if step == STEPS - 1 and nxt is not None:
                        pe.wait_ge(freeA, AT_STAGE["k_T", nxt][0] + 1)
                    if step == 0 and j == 1:
                        pe.wait_ge(loaded["late"], 64)
                    one_step(j, step, step % 2, prev, nxt)
                    for name, t in stages(j, step):
                        stage(name, t)
            pv(TILES - 1, TOTAL - 1, STEPS - 1, 1)
            for name, t in TAIL:
                stage(name, t)

        @block.scalar
        def _(act):
            act.dma_start(c_sb[:], c_t).then_inc(loaded["mod"], 16)
            act.dma_start(wmod_sb[:], wmod).then_inc(loaded["mod"], 16)
            act.dma_start(mask_sb[:], mask).then_inc(loaded["consts"], 16)
            act.dma_start(cosk_sb[:], cos_k.rearrange("(j p) d -> p j d", p=T)).then_inc(loaded["tables"], 16)
            act.dma_start(sink_sb[:], sin_k.rearrange("(j p) d -> p j d", p=T)).then_inc(loaded["tables"], 16)

            def turn_queries(s, b):
                act.wait_ge(q_turned, s + 1)
                nc.scalar.copy(qT[b][:].rearrange("p h t -> p (h t)"), q_ps[:, 0:2 * T]).then_inc(qT_ready, 1)

            def keep_probs(j, s, step, b, h):
                a, _ = bank_counts(j, step)
                if uses(j) == 1 and h == 1:
                    return
                cols = min(blocks(j), 4) * T
                act.wait_ge(fullA, a + (h + 1))
                if not (isinstance(s, int) and s < 2):
                    act.wait_ge(pv_done, s - 1)
                nc.scalar.copy(PT[b][h][:, 0:cols], bankA[:, 0:cols]).then_inc(freeA, 1)

            def exponential(j, s, hp, b, h, turned):
                act.wait_ge(least_ready[h], s + 1)
                if turned is not None:
                    act.wait_ge(turned[0], turned[1])
                nc.scalar.activation(P[h][:, 0:blocks(j) * T], S[h][:, 0:blocks(j) * T], ACT.Exp,
                                     bias=least[:, h:h + 1], scale=-1.0,
                                     accum_out=sums[j % 2][:].rearrange("p b h -> p (b h)")
                                     [:, bass.ds(hp * 2 + (b * HEADS + h), 1)]).then_inc(probs[h], 1)

            def one_step(j, step, b, nxt, nxt_hp):
                s = step + j * STEPS
                if nxt is not None and not (isinstance(s, int) and s + 2 >= TOTAL):
                    turn_queries(s + 2, b)
                a, bb = bank_counts(j, step)
                for h in range(2):
                    keep_probs(j, s, step, b, h)
                    if nxt is not None:
                        if uses(j) == 1:
                            turned = ((fullA, a + 1), (fullB, bb + 1))[h]
                        else:
                            turned = (fullB, bb + (h + 1))
                        exponential(nxt, s + 1, nxt_hp, 1 - b, h, turned)

            def stage(name, t):
                a, b = AT_STAGE[name, t]
                if name == "norm1_T":
                    act.wait_ge(fullA, a + 1)
                    if t == 0:
                        act.wait_ge(mod_ready, 1)
                    for i in range(B):
                        last = nc.scalar.activation(h1T[:, i, :], bankA[:, i * T:(i + 1) * T], ACT.Identity,
                                                    bias=mod_cols[:, 0, i:i + 1], scale=mod_cols[:, 1, i:i + 1])
                    last.then_inc(freeA, 1)
                elif name == "norm2_T":
                    act.wait_ge(fullB, b + 1)
                    for i in range(B):
                        last = nc.scalar.activation(h2T[:, t % 2, i, :], bankB[:, i * T:(i + 1) * T], ACT.Identity,
                                                    bias=mod_cols[:, 2, i:i + 1], scale=mod_cols[:, 3, i:i + 1])
                    last.then_inc(freeB, 1)
                elif name == "k_T":
                    act.wait_ge(fullA, a + 1)
                    nc.scalar.copy(k_stack[:, :, :, t * T:(t + 1) * T],
                                   bankA[:].rearrange("p (s b t) -> p s b t", s=2, b=B)).then_inc(freeA, 1)
                elif name == "router":
                    act.wait_ge(sorted_ready, t + 1)
                    for i in range(B):
                        last = nc.scalar.activation(e_sorted[:, i, :], sorted_l[:, i, :], ACT.Exp,
                                                    bias=neg_top[:, i:i + 1], accum_out=e_sum[:, i:i + 1])
                    last.then_inc(router_exp, 1)

            act.wait_ge(loaded["mod"], 32)
            nc.scalar.activation(silu[:, 0, :], c_sb[:], ACT.Exp, scale=-1.0).then_inc(silu_exp, 1)
            act.wait_ge(loaded["consts"], 32)
            nc.scalar.copy(ident_bf[:], ident_sb[:])
            nc.scalar.copy(mask_bf[:], mask_sb[:]).then_inc(masks_ready, 1)
            for name, t in HEAD:
                stage(name, t)
            turn_queries(0, 0)
            turn_queries(1, 1)
            for h in range(2):
                exponential(0, 0, 0, 0, h, None)
            for j in range(TILES):
                for step in list(range(LOOP_FROM)) + [None] + list(range(LOOP_TO, STEPS)):
                    if step is None:
                        with act.Fori(LOOP_FROM // 2, LOOP_TO // 2) as hp:
                            for b in range(B):
                                one_step(j, hp * 2 + b, b, j, hp + b)
                        continue
                    nxt = j if step < STEPS - 1 else (j + 1 if j + 1 < TILES else None)
                    nxt_hp = (step + 1) // 2 % PAIRS
                    one_step(j, step, step % 2, nxt, nxt_hp)
                    for name, t in stages(j, step):
                        stage(name, t)
            for name, t in TAIL:
                stage(name, t)

        @block.vector
        def _(dve):
            links = [0]

            def link(ins):
                links[0] += 1
                ins.then_inc(dve_link, 1)
                dve.wait_ge(dve_link, links[0])

            def smallest(j, s, h):
                dve.wait_ge(scores[h], s + 1)
                nc.vector.tensor_reduce(least[:, h:h + 1], S[h][:, 0:blocks(j) * T], AX.X, ALU.min)\
                    .then_inc(least_ready[h], 1)

            def keep_probs(j, s, step, b, h):
                _, bc = bank_counts(j, step)
                if uses(j) == 1 and h == 0:
                    return
                first = 0 if uses(j) == 1 else 4
                cols = (blocks(j) - first) * T
                count = bc + 1 if uses(j) == 1 else bc + (h + 1)
                dve.wait_ge(fullB, count)
                if not (isinstance(s, int) and s < 2):
                    dve.wait_ge(pv_done, s - 1)
                nc.vector.tensor_copy(PT[b][h][:, first * T:first * T + cols], bankB[:, 0:cols]).then_inc(freeB, 1)

            def keep_output(j, s, hp, b):
                dve.wait_ge(pv_done, s + 1)
                nc.vector.tensor_copy(oT[j % 2][:, b].rearrange("p h t -> p (h t)")[:, bass.ds(hp * T, T)],
                                      o_ps[:, 0:T]).then_inc(o_free, 1)

            def one_step(j, step, b, nxt, prev, prev_hp):
                s = step + j * STEPS
                for h in range(2):
                    if nxt is not None:
                        smallest(nxt, s + 1, h)
                    keep_probs(j, s, step, b, h)
                if prev is not None:
                    keep_output(prev, s - 1, prev_hp, 1 - b)

            def norm_stats(tiles, stats_, mean_var_):
                for i in range(B):
                    last = nc.vector.bn_stats(stats_[:, i, :], tiles[:, i, :])
                link(last)
                for i in range(B):
                    last = nc.vector.bn_aggr(mean_var_[:, i, :], stats_[:, i, :])
                last.then_inc(stats_ready, 1)

            def normalise(tiles, dst, mean_var_, rstd_, ready):
                for i in range(B):
                    last = nc.vector.tensor_scalar(dst[:, i, :], tiles[:, i, :], mean_var_[:, i, 0:1],
                                                   rstd_[:, i:i + 1], ALU.subtract, ALU.mult)
                last.then_inc(ready, 1)

            def norm1_stats(t):
                if t < TILES:
                    norm_stats(x_sb[:, :, t, :], stats, mean_var)

            def norm1(t):
                if t < TILES:
                    dve.wait_ge(rstd_ready, RSTD[1, t])
                    if t >= 1:
                        dve.wait_ge(fullA, AT_STAGE["norm1_T", t - 1][0] + 1)
                    normalise(x_sb[:, :, t, :], normed1, mean_var, rstd, normed1_ready)

            def norm2_stats(t):
                dve.wait_ge(x1_ready, t + 1)
                norm_stats(x_sb[:, :, t, :], stats2, mean_var2)

            def norm2(t):
                dve.wait_ge(rstd_ready, RSTD[2, t])
                normalise(x_sb[:, :, t, :], normed2, mean_var2, rstd2, normed2_ready)

            def rope(parts, dst_cos, dst_sin, cos, sin, heads):
                shape = [T, heads, DH]
                nc.vector.tensor_tensor(dst_cos, parts, cos.unsqueeze(1).to_broadcast(shape), ALU.mult)
                half = [T, heads, HALF]
                nc.vector.tensor_tensor(dst_sin[:, :, 0:HALF], parts[:, :, HALF:DH],
                                        sin[:, 0:HALF].unsqueeze(1).to_broadcast(half), ALU.mult)
                return nc.vector.tensor_tensor(dst_sin[:, :, HALF:DH], parts[:, :, 0:HALF],
                                               sin[:, HALF:DH].unsqueeze(1).to_broadcast(half), ALU.mult)

            def stage(name, t):
                a, b = AT_STAGE[name, t]
                if name == "kv":
                    dve.wait_ge(fullB, b + 1)
                    kv = bankB[:, 0:B * 2 * DH].rearrange("p (b d) -> p b d", b=B)
                    nc.vector.tensor_copy(v_sb[:, :, t, :], kv[:, :, DH:2 * DH])
                    if t >= 1:
                        dve.wait_ge(k_ready, t)
                    rope(kv[:, :, 0:DH], k_cos[:], k_sin[:], cosk_sb[:, t, :], sink_sb[:, t, :], B).then_inc(freeB, 1)
                elif name in ("q0", "q1"):
                    i = int(name[1])
                    for c, (bank_, full, free, count) in enumerate(((bankA, fullA, freeA, a), (bankB, fullB, freeB, b))):
                        n = 4 * t + 2 * i + c
                        dve.wait_ge(full, count + 1)
                        if n >= 2:
                            dve.wait_ge(q_ready, n - 1)
                        rope(bank_[:].rearrange("p (h d) -> p h d", d=DH), rope_cos[:, c], rope_sin[:, c],
                             cosq_sb[:, t, :], sinq_sb[:, t, :], 8).then_inc(free, 1)
                elif name == "recip_T":
                    for i in range(B):
                        for half, (bank_, full, free, count) in enumerate(
                                ((bankA, fullA, freeA, a + i), (bankB, fullB, freeB, b + i))):
                            dve.wait_ge(full, count + 1)
                            hs = slice(4 * half, 4 * half + 4)
                            nc.vector.tensor_tensor(oT_n[:, i, hs, :], oT[t % 2][:, i, hs, :],
                                                    bank_[:].rearrange("p (h t) -> p h t", h=4), ALU.mult)\
                                .then_inc(free, 1)
                elif name == "wo":
                    dve.wait_ge(fullA, a + 1)
                    nc.vector.tensor_tensor(attn[:], bankA[:, 0:B * DIM].rearrange("p (b d) -> p b d", b=B),
                                            gates[:, 0], ALU.mult).then_inc(freeA, 1)
                elif name == "router":
                    dve.wait_ge(fullA, a + 1)
                    nc.vector.tensor_copy(logits[:], bankA[:, 0:B * EXPERTS].rearrange("p (b e) -> p b e", b=B))\
                        .then_inc(freeA, 1)
                    dve.wait_ge(freeA, a + 1)
                    for i in range(B):
                        last = nc.vector.max(sorted_l[:, i, :], logits[:, i, :])
                    link(last)
                    nc.vector.tensor_scalar(neg_top[:], sorted_l[:, :, 0], -1.0, None, ALU.mult).then_inc(sorted_ready, 1)
                    for i in range(B):
                        last = nc.vector.max_index(top_idx[:, i, :], sorted_l[:, i, :], logits[:, i, :])
                    link(last)
                    link(nc.vector.tensor_copy(top_idx_f[:], top_idx[:]))
                elif name == "comb_T":
                    dve.wait_ge(fullB, b + 1)
                    nc.vector.tensor_copy(combT[:], bankB[0:EXPERTS, 0:B * T].rearrange("p (b t) -> p b t", b=B))\
                        .then_inc(freeB, 1)
                elif name in ("ffn0", "ffn1"):
                    i = int(name[3])
                    if t >= 1:
                        dve.wait_ge(out_ready, B * (t - 1) + i + 1)
                    dve.wait_ge(fullA, a + 1)
                    nc.vector.tensor_copy(y[i][:, 0, :], bankA[:, 0:DIM]).then_inc(freeA, 1)
                    dve.wait_ge(freeA, a + 1)
                    at = 0
                    for bank_, full, free, count, c in ((bankB, fullB, freeB, b, 0), (bankA, fullA, freeA, a + 1, 1)):
                        dve.wait_ge(full, count + 1)
                        for e in range(4):
                            ins = nc.vector.scalar_tensor_tensor(
                                out=y[i][:, 1 - at, :], in0=bank_[:, e * DIM:(e + 1) * DIM],
                                scalar=comb[:, i, 4 * c + e:4 * c + e + 1], in1=y[i][:, at, :],
                                op0=ALU.mult, op1=ALU.add)
                            at = 1 - at
                            if e == 3:
                                ins.then_inc(free, 1)
                                dve.wait_ge(free, count + 1)
                            else:
                                link(ins)
                    nc.vector.tensor_tensor(y[i][:, 1, :], y[i][:, 0, :], gates[:, 1, i, :], ALU.mult).then_inc(y_ready, 1)

            def reciprocals(t):
                dve.wait_ge(probs[0], STEPS * (t + 1))
                dve.wait_ge(probs[1], STEPS * (t + 1))
                if t >= 1:
                    dve.wait_ge(rows_ready, t)
                nc.vector.reciprocal(recips[:], sums[t % 2][:]).then_inc(recips_ready, 1)

            def combine_weights(t):
                dve.wait_ge(router_exp, t + 1)
                link(nc.vector.reciprocal(e_rec[:], e_sum[:]))
                link(nc.vector.tensor_tensor(top_w[:], e_sorted[:, :, 0:TOPK],
                                             e_rec[:].unsqueeze(2).to_broadcast([T, B, TOPK]), ALU.mult))
                for i in range(B):
                    for k in range(TOPK):
                        last = nc.vector.tensor_scalar(comb_k[:, i, k, :], iota_sb[:], top_idx_f[:, i, k:k + 1],
                                                       top_w[:, i, k:k + 1], ALU.is_equal, ALU.mult)
                link(last)
                if t >= 1:
                    dve.wait_ge(y_ready, B * t)
                nc.vector.tensor_tensor(comb[:], comb_k[:, :, 0, :], comb_k[:, :, 1, :], ALU.add).then_inc(comb_ready, 1)

            dve.wait_ge(silu_exp, 1)
            link(nc.vector.tensor_scalar_add(silu[:, 1, :], silu[:, 0, :], 1.0))
            link(nc.vector.reciprocal(silu[:, 0, :], silu[:, 1, :]))
            link(nc.vector.tensor_tensor(silu[:, 2, :], silu[:, 0, :], c_sb[:], ALU.mult))
            nc.vector.tensor_copy(silu_rows[:], silu[:, 2, :].unsqueeze(2).to_broadcast([DIM, B, T])).then_inc(silu_ready, 1)
            dve.wait_ge(loaded["x0"], 16 * B)
            norm1_stats(0)
            norm1(0)
            dve.wait_ge(fullA, 1)
            cols = bankA[:, 0:4 * B].rearrange("p (m b) -> p m b", b=B)
            nc.vector.tensor_copy(mod_cols[:, 0:4:2, :], cols[:, 0:4:2, :])
            nc.vector.tensor_scalar_add(mod_cols[:, 1:4:2, :], cols[:, 1:4:2, :], 1.0).then_inc(freeA, 1)
            dve.wait_ge(fullB, 1)
            link(nc.vector.tensor_scalar(gate_tmp[:, 0, :], bankB[:], -1.0, None, ALU.mult))
            link(nc.vector.tensor_tensor(gate_tmp[:, 1, :], bankB[:], gate_tmp[:, 0, :], ALU.max))
            link(nc.vector.tensor_scalar(gate_tmp[:, 0, :], bankB[:], 0.0, 2.0, ALU.is_ge, ALU.mult))
            nc.vector.tensor_scalar(gate_tmp[:, 0, :], gate_tmp[:, 0, :], -1.0, None, ALU.add).then_inc(freeB, 1)
            link(nc.vector.tensor_scalar(gate_tmp[:, 1, :], gate_tmp[:, 1, :], 0.25, None, ALU.max))
            dve.wait_ge(freeB, 1)
            nc.vector.tensor_tensor(gates[:].rearrange("p g b d -> p (g b d)"), gate_tmp[:, 0, :],
                                    gate_tmp[:, 1, :], ALU.mult).then_inc(mod_ready, 1)
            dve.wait_ge(loaded["tables"], 64)
            dve.wait_ge(consts_ready, 1)
            for name, t in HEAD:
                stage(name, t)
            norm1_stats(1)
            norm1(1)
            for h in range(2):
                smallest(0, 0, h)
            for j in range(TILES):
                for step in list(range(LOOP_FROM)) + [None] + list(range(LOOP_TO, STEPS)):
                    if step is None:
                        with dve.Fori(LOOP_FROM // 2, LOOP_TO // 2) as hp:
                            for b in range(B):
                                one_step(j, hp * 2 + b, b, j, j, hp - (1 - b))
                        continue
                    prev = j if step else (j - 1 if j else None)
                    prev_hp = (step - 1) // 2 if step else PAIRS - 1
                    nxt = j if step < STEPS - 1 else (j + 1 if j + 1 < TILES else None)
                    one_step(j, step, step % 2, nxt, prev, prev_hp)
                    if step == 0:
                        if j >= 1:
                            reciprocals(j - 1)
                        if j >= 2:
                            norm2_stats(j - 2)
                    if step == 1 and j >= 2:
                        norm2(j - 2)
                    if step == 3 and j >= 2:
                        combine_weights(j - 2)
                    for name, t in stages(j, step):
                        stage(name, t)
                    if step == 3:
                        if j == 0:
                            dve.wait_ge(loaded["x1"], 16 * B)
                        norm1_stats(j + 2)
                    if step == LOOP_TO:
                        norm1(j + 2)
            keep_output(TILES - 1, TOTAL - 1, PAIRS - 1, 1)
            reciprocals(TILES - 1)
            dve.wait_ge(recips_ready, TILES)
            dve.wait_ge(fullB, AT_STAGE["recip_T", TILES - 2][1] + 2)
            nc.vector.tensor_copy(recip_rows[:].rearrange("p b (h d) -> p (b h) d", d=DH),
                                  recips[:].rearrange("p b h -> p (b h)").unsqueeze(2)
                                  .to_broadcast([T, B * HEADS, DH])).then_inc(rows_ready, 1)
            norm2_stats(TILES - 2)
            norm2(TILES - 2)
            for name, t in TAIL:
                if name == "comb_T":
                    combine_weights(t)
                stage(name, t)
                if (name, t) == ("comb_T", TILES - 2):
                    norm2_stats(TILES - 1)
                    norm2(TILES - 1)

        @block.gpsimd
        def _(pool):
            links = [0]

            def link(ins):
                links[0] += 1
                ins.then_inc(pool_link, 1)
                pool.wait_ge(pool_link, links[0])

            def inverse_deviation(count, mean_var_, var_eps_, rstd_):
                pool.wait_ge(stats_ready, count)
                link(nc.gpsimd.tensor_scalar(var_eps_[:], mean_var_[:, :, 1], EPS, None, ALU.add))
                nc.gpsimd.tensor_tensor(rstd_[:], var_eps_[:], minus_half[:], ALU.pow).then_inc(rstd_ready, 1)

            def keys(t):
                pool.wait_ge(freeB, AT_STAGE["kv", t][1] + 1)
                if t >= 1:
                    pool.wait_ge(fullA, AT_STAGE["k_T", t - 1][0] + 1)
                link(nc.gpsimd.tensor_tensor(k_cos[:], k_cos[:], k_sin[:], ALU.add))
                nc.gpsimd.tensor_copy(k_split[:, :, 2, :], k_cos[:])
                link(nc.gpsimd.tensor_copy(k_split[:, :, 0, :], k_cos[:]))
                nc.gpsimd.tensor_tensor(k_split[:, :, 1, :], k_cos[:], k_split[:, :, 0, :].bitcast(f32),
                                        ALU.subtract).then_inc(k_ready, 1)

            def query_chunks(t, i):
                a, b = AT_STAGE[f"q{i}", t]
                if t >= 2:
                    pool.wait_ge(q_turned, STEPS * (t - 1))
                for c, (free, count) in enumerate(((freeA, a), (freeB, b))):
                    n = 4 * t + 2 * i + c + 1
                    pool.wait_ge(free, count + 1)
                    nc.gpsimd.tensor_tensor(rope_cos[:, c], rope_cos[:, c], rope_sin[:, c], ALU.add).then_inc(rope_sum, 1)
                    pool.wait_ge(rope_sum, n)
                    nc.gpsimd.tensor_copy(q_split[:, t % 2, i, 8 * c:8 * c + 8, 0, :], rope_cos[:, c]).then_inc(rope_high, 1)
                    pool.wait_ge(rope_high, n)
                    nc.gpsimd.tensor_tensor(q_split[:, t % 2, i, 8 * c:8 * c + 8, 1, :], rope_cos[:, c],
                                            q_split[:, t % 2, i, 8 * c:8 * c + 8, 0, :].bitcast(f32),
                                            ALU.subtract).then_inc(q_ready, 1)

            def rows(t):
                pool.wait_ge(recips_ready, t + 1)
                if t >= 1:
                    pool.wait_ge(fullB, AT_STAGE["recip_T", t - 1][1] + 2)
                nc.gpsimd.tensor_copy(recip_rows[:].rearrange("p b (h d) -> p (b h) d", d=DH),
                                      recips[:].rearrange("p b h -> p (b h)").unsqueeze(2)
                                      .to_broadcast([T, B * HEADS, DH])).then_inc(rows_ready, 1)

            def residual(t):
                pool.wait_ge(freeA, AT_STAGE["wo", t][0] + 1)
                nc.gpsimd.tensor_tensor(x_sb[:, :, t, :], x_sb[:, :, t, :], attn[:], ALU.add).then_inc(x1_ready, 1)

            def result(t, i):
                pool.wait_ge(y_ready, B * t + i + 1)
                if t >= 1:
                    pool.wait_ge(stored, 16 * B * t)
                nc.gpsimd.tensor_tensor(out_sb[i][:], y[i][:, 1, :], x_sb[:, i, t, :], ALU.add).then_inc(out_ready, 1)

            link(nc.gpsimd.memset(minus_half[:], -0.5))
            nc.gpsimd.iota(iota_sb[:], pattern=[[1, EXPERTS]], base=0, channel_multiplier=0,
                           allow_small_or_imprecise_dtypes=True).then_inc(consts_ready, 1)
            inverse_deviation(RSTD[1, 0], mean_var, var_eps, rstd)
            keys(0)
            query_chunks(0, 0)
            query_chunks(0, 1)
            inverse_deviation(RSTD[1, 1], mean_var, var_eps, rstd)
            for j in range(TILES):
                if j >= 2:
                    inverse_deviation(RSTD[2, j - 2], mean_var2, var_eps2, rstd2)
                if j + 1 < TILES:
                    keys(j + 1)
                    query_chunks(j + 1, 0)
                    query_chunks(j + 1, 1)
                if j + 2 < TILES:
                    inverse_deviation(RSTD[1, j + 2], mean_var, var_eps, rstd)
                if j >= 1:
                    rows(j - 1)
                if j >= 2:
                    result(j - 2, 0)
                if j >= 1:
                    residual(j - 1)
                if j >= 2:
                    result(j - 2, 1)
            inverse_deviation(RSTD[2, TILES - 2], mean_var2, var_eps2, rstd2)
            residual(TILES - 1)
            inverse_deviation(RSTD[2, TILES - 1], mean_var2, var_eps2, rstd2)
            for t in (TILES - 2, TILES - 1):
                for i in range(B):
                    result(t, i)


def rope_tables():
    inv_freq = (1.0 / np.power(np.float32(10000.0), np.arange(0, DH, 2, dtype=np.float32) / np.float32(DH))).astype(np.float32)
    freqs = np.arange(N, dtype=np.float32)[:, None] * inv_freq[None, :]
    cos = np.cos(np.concatenate([freqs, freqs], axis=1)).astype(np.float32)
    sin = np.sin(np.concatenate([-freqs, freqs], axis=1)).astype(np.float32)
    s = np.float32(-SCALE)
    return cos * s, sin * s, cos, sin


def kernel(L0_attn_x, L0_attn_Wq, L0_attn_Wkv, L0_attn_Wo, L0_ffn_gate_w, L0_ffn_expert_w, L0_ffn_expert_b,
           L0_c, L0_wmod):
    import concourse.bacc as bacc
    from concourse.bass_utils import run_bass_kernel_spmd

    cos_q, sin_q, cos_k, sin_k = rope_tables()
    later = np.arange(T)[None, :] > np.arange(T)[:, None]
    arrays = {
        "x": L0_attn_x, "wq": L0_attn_Wq, "wkv": L0_attn_Wkv, "wo": L0_attn_Wo,
        "gate": np.transpose(L0_ffn_gate_w),
        "expert_w": np.transpose(L0_ffn_expert_w, (2, 0, 1)).reshape(DIM, EXPERTS * DIM),
        "expert_b": L0_ffn_expert_b, "c_t": np.transpose(L0_c), "wmod": L0_wmod,
        "cos_q": cos_q, "sin_q": sin_q, "cos_k": cos_k, "sin_k": sin_k,
        "ident": np.eye(T, dtype=np.float32),
        "mask": np.where(later, np.float32(MASKED), np.float32(0.0)),
    }
    arrays = {k: np.ascontiguousarray(v) for k, v in arrays.items()}
    nc = bacc.Bacc("TRN2", target_bir_lowering=False, num_devices=1)
    aps = [nc.dram_tensor(f"{k}_dram", v.shape, mybir.dt.from_np(v.dtype), kind="ExternalInput").ap()
           for k, v in arrays.items()]
    out = nc.dram_tensor("out_dram", (B, N, DIM), mybir.dt.float32, kind="ExternalOutput").ap()
    build(nc, *aps, out)
    r = run_bass_kernel_spmd(nc, [{f"{k}_dram": v for k, v in arrays.items()}], core_ids=[0])
    return r.results[0]["out_dram"]
```

```python
import numpy as np
import concourse.bass as bass
from concourse import mybir
from contextlib import ExitStack


B, N, DIM = 2, 1024, 128
HEADS, DH = 16, 64
HALF = DH // 2
EXPERTS, TOPK = 8, 2
T = 128
TILES = N // T
PAIRS = HEADS // 2
STEPS = PAIRS * B
TOTAL = TILES * STEPS
BANK = 512
SCALE = float(DH) ** -0.5
EPS = 1e-5
MASKED = 3.0e38
SA, CA, GA, SB, CB, GB = range(6)

LOOPS = ((2, 8), (10, 14))


def blocks(j):
    return j + 1


def uses(j):
    return 1 if blocks(j) <= 4 else 2


def stages(j, step):
    table = {
        0: [("kv", j + 1), ("comb_T", j - 2)],
        1: [("recip_T", j - 1), ("bias", j - 2)],
        8: [("norm1_T", j + 2), ("wo", j - 1)],
        9: [("k_T", j + 1)],
        14: [("norm2_T", j - 1)],
        15: [("router", j - 1)],
    }
    return [(name, t) for name, t in table.get(step, []) if 0 <= t < TILES]


HEAD = [("norm1_T", 0), ("kv", 0), ("q_first", 0), ("q_second", 0), ("k_T", 0), ("norm1_T", 1)]
TAIL = [("comb_T", TILES - 2), ("recip_T", TILES - 1), ("bias", TILES - 2), ("wo", TILES - 1),
        ("ffn0", TILES - 2), ("ffn1", TILES - 2), ("norm2_T", TILES - 1), ("router", TILES - 1),
        ("comb_T", TILES - 1), ("bias", TILES - 1), ("ffn0", TILES - 1), ("ffn1", TILES - 1)]
FILLS = {"norm1_T": (1, 0), "kv": (0, 1), "q_first": (1, 1), "q_second": (1, 1), "k_T": (1, 0),
         "recip_T": (2, 2), "wo": (1, 0), "norm2_T": (0, 1), "router": (1, 0), "comb_T": (0, 1),
         "bias": (1, 0), "ffn0": (1, 1), "ffn1": (1, 1)}


def ledger():
    a, b = 1, 1
    at_step, at_stage = {}, {}

    def stage(name, t):
        nonlocal a, b
        at_stage[name, t] = (a, b)
        a, b = a + FILLS[name][0], b + FILLS[name][1]

    for name, t in HEAD:
        stage(name, t)
    for j in range(TILES):
        for step in range(STEPS):
            at_step[j, step] = (a, b)
            a, b = a + uses(j), b + uses(j)
            for name, t in stages(j, step):
                stage(name, t)
    for name, t in TAIL:
        stage(name, t)
    return at_step, at_stage


AT_STEP, AT_STAGE = ledger()

RSTD = {(1, 0): 1, (1, 1): 2}
for _j in range(TILES):
    if _j + 2 < TILES:
        RSTD[1, _j + 2] = len(RSTD) + 1
    if _j >= 1:
        RSTD[2, _j - 1] = len(RSTD) + 1
RSTD[2, TILES - 1] = len(RSTD) + 1


def bank_counts(j, step):
    if isinstance(step, tuple):
        step, first = step
        a, b = AT_STEP[j, first]
        return (step - first) * uses(j) + a, (step - first) * uses(j) + b
    return AT_STEP[j, step]


def plan(j):
    steps, at = [], 0
    for first, end in LOOPS:
        steps += list(range(at, first)) + [(first, end)]
        at = end
    return steps + list(range(at, STEPS))


def score_chunks(j):
    width = blocks(j) * T
    if width % BANK == T and width > BANK:
        return T, [(0, BANK - T), (BANK - T, width)]
    return 0, [(c, min(c + BANK, width)) for c in range(0, width, BANK)]


def build(nc, x, wq, wkv, wo, gate, expert_w, expert_b, c_t, wmod,
          cos_q, sin_q, cos_k, sin_k, ident, mask, out):
    f32, f32r, bf16, u32 = mybir.dt.float32, mybir.dt.float32r, mybir.dt.bfloat16, mybir.dt.uint32
    ALU, ACT, AX = mybir.AluOpType, mybir.ActivationFunctionType, mybir.AxisListType

    ctx = ExitStack()
    with ctx:
        def sb(name, shape, dt=f32):
            return ctx.enter_context(nc.sbuf_tensor(name, shape, dt))

        def bank(name, shape):
            return ctx.enter_context(nc.psum_tensor(name, shape, f32))

        def sem(name):
            return ctx.enter_context(nc.semaphore(name))

        x_sb = sb("x_sb", [T, B, TILES, DIM])
        wq_sb = sb("wq_sb", [DIM, HEADS * DH])
        wkv_sb = sb("wkv_sb", [DIM, 2 * DH])
        wo_sb = sb("wo_sb", [2 * DH, PAIRS, DIM])
        we_sb = sb("we_sb", [DIM, EXPERTS * DIM])
        gate_sb = sb("gate_sb", [DIM, EXPERTS])
        eb_sb = sb("eb_sb", [EXPERTS, DIM])
        wmod_sb = sb("wmod_sb", [DIM, 6 * DIM])
        c_sb = sb("c_sb", [DIM, B])
        cosq_sb, sinq_sb, cosk_sb, sink_sb = (sb(n, [T, TILES, DH]) for n in ("cosq", "sinq", "cosk", "sink"))
        ident_sb = sb("ident_sb", [T, T])
        mask_sb = sb("mask_sb", [T, T])
        ident_r = sb("ident_r", [T, T], f32r)
        ident_bf = sb("ident_bf", [T, T], bf16)
        mask_bf = sb("mask_bf", [T, T], bf16)
        minus_half = sb("minus_half", [T, B])
        iota_sb = sb("iota_sb", [T, EXPERTS])
        silu = sb("silu", [DIM, 3, B])
        silu_rows = sb("silu_rows", [DIM, B, T])
        mod_cols = sb("mod_cols", [DIM, 4, B])
        gates = sb("gates", [T, 2, B, DIM])
        gate_tmp = sb("gate_tmp", [T, 3, 2 * B * DIM])
        stats = sb("stats", [T, B, 6])
        mean_var = sb("mean_var", [T, B, 2])
        var_eps = sb("var_eps", [T, B])
        rstd = sb("rstd", [T, B])
        normed1 = sb("normed1", [T, B, DIM])
        stats2 = sb("stats2", [T, B, 6])
        mean_var2 = sb("mean_var2", [T, B, 2])
        var_eps2 = sb("var_eps2", [T, B])
        rstd2 = sb("rstd2", [T, B])
        normed2 = sb("normed2", [T, B, DIM])
        h1T = sb("h1T", [DIM, 2, B, T])
        h2T = sb("h2T", [DIM, 2, B, T])
        k_split = sb("k_split", [T, B, 3, DH], f32r)
        k_cos = sb("k_cos", [T, B, DH])
        k_sin = sb("k_sin", [T, B, DH])
        k_stack = sb("k_stack", [2 * DH, 2, B, N], f32r)
        v_sb = sb("v_sb", [T, B, TILES, DH])
        rope_cos = sb("rope_cos", [T, B, 2, DH])
        rope_sin = sb("rope_sin", [T, B, 2, DH])
        wide_cos = sb("wide_cos", [T, 2, HEADS // 2, DH])
        wide_sin = sb("wide_sin", [T, 2, HEADS // 2, DH])
        q_split = sb("q_split", [T, 2, B, PAIRS, 2, 2, DH], f32r)
        q_feed = [sb(f"q_feed{i}", [T, 2, 2 * DH], f32r) for i in range(2)]
        qT = [sb(f"qT{i}", [2 * DH, 2, T], f32r) for i in range(2)]
        least = sb("least", [T, 2])
        P = [sb(f"P{i}", [T, N]) for i in range(2)]
        PT = [[sb(f"PT{i}{h}", [T, N]) for h in range(2)] for i in range(2)]
        sums = [sb(f"sums{i}", [T, B, HEADS]) for i in range(2)]
        recips = sb("recips", [T, B, HEADS])
        recip_rows = sb("recip_rows", [T, B, HEADS * DH])
        oT = [sb(f"oT{i}", [2 * DH, B, PAIRS, T]) for i in range(2)]
        oT_n = sb("oT_n", [2 * DH, B, PAIRS, T])
        attn = sb("attn", [T, B, DIM])
        logits = sb("logits", [T, B, EXPERTS])
        sorted_l = sb("sorted_l", [T, B, 8])
        neg_top = sb("neg_top", [T, B])
        e_sorted = sb("e_sorted", [T, B, 8])
        e_sum = sb("e_sum", [T, B])
        e_rec = sb("e_rec", [T, B])
        top_idx = sb("top_idx", [T, B, 8], u32)
        top_idx_f = sb("top_idx_f", [T, B, 8])
        top_w = sb("top_w", [T, B, TOPK])
        comb_k = sb("comb_k", [T, B, TOPK, EXPERTS])
        comb = sb("comb", [T, B, EXPERTS])
        combT = sb("combT", [EXPERTS, B, T])
        y = [sb(f"y{b}", [T, DIM]) for b in range(B)]
        y_gated = [sb(f"y_gated{b}", [T, DIM]) for b in range(B)]
        out_sb = [sb(f"out_sb{b}", [T, DIM]) for b in range(B)]

        S = [bank(f"S{h}", [T, N]) for h in range(2)]
        bankA = bank("bankA", [T, BANK])
        bankB = bank("bankB", [T, BANK])
        o_ps = bank("o_ps", [T, BANK])
        q_ps = bank("q_ps", [T, BANK])
        o_out, o_query, o_expert = (o_ps[:, i * T:(i + 1) * T] for i in range(3))

        def halves_swapped(columns):
            (pitch, parts), (_, n) = columns.ap
            return bass.AP(tensor=columns.tensor, offset=columns.offset + HALF,
                           ap=[[pitch, parts], [DH, n // DH], [-HALF, 2], [1, HALF]])

        loaded = {n: sem(f"loaded_{n}") for n in ("x0", "x1", "mod", "tables", "consts", "w", "late")}
        masks_ready = sem("masks_ready")
        consts_ready = sem("consts_ready")
        silu_exp = sem("silu_exp")
        silu_ready = sem("silu_ready")
        stats_ready = sem("stats_ready")
        rstd_ready = sem("rstd_ready")
        normed1_ready = sem("normed1_ready")
        normed2_ready = sem("normed2_ready")
        fullA, fullB = sem("fullA"), sem("fullB")
        freeA, freeB = sem("freeA"), sem("freeB")
        k_parts = sem("k_parts")
        k_ready = sem("k_ready")
        wide_parts, wide_sum, wide_high = sem("wide_parts"), sem("wide_sum"), sem("wide_high")
        wide_ready = sem("wide_ready")
        rope_parts = sem("rope_parts")
        rope_sum = sem("rope_sum")
        rope_high = sem("rope_high")
        q_ready = sem("q_ready")
        q_fed = [sem(f"q_fed{i}") for i in range(2)]
        q_turned = sem("q_turned")
        qT_ready = sem("qT_ready")
        scores = [sem("scores_even"), sem("scores_odd")]
        least_ready = [sem("least_even"), sem("least_odd")]
        probs = [sem("probs_even"), sem("probs_odd")]
        o_full = sem("o_full")
        o_free = sem("o_free")
        recips_ready = sem("recips_ready")
        rows_ready = sem("rows_ready")
        attn_ready = sem("attn_ready")
        x1_ready = sem("x1_ready")
        sorted_ready = sem("sorted_ready")
        router_exp = sem("router_exp")
        comb_ready = sem("comb_ready")
        y_added = sem("y_added")
        y_ready = sem("y_ready")
        out_ready = sem("out_ready")
        stored = sem("stored")
        dve_link, pool_link = sem("dve_link"), sem("pool_link")

        block = ctx.enter_context(nc.Block())

        @block.sync
        def _(sp):
            x_v = x.rearrange("b (j p) d -> p b j d", p=T)
            for b in range(B):
                sp.dma_start(x_sb[:, b, 0:2, :], x_v[:, b, 0:2, :]).then_inc(loaded["x0"], 16)
            sp.dma_start(ident_sb[:], ident).then_inc(loaded["consts"], 16)
            sp.dma_start(wkv_sb[:], wkv).then_inc(loaded["w"], 16)
            sp.dma_start(wq_sb[:], wq).then_inc(loaded["w"], 16)
            sp.dma_start(cosq_sb[:], cos_q.rearrange("(j p) d -> p j d", p=T)).then_inc(loaded["tables"], 16)
            sp.dma_start(sinq_sb[:], sin_q.rearrange("(j p) d -> p j d", p=T)).then_inc(loaded["tables"], 16)
            for b in range(B):
                sp.dma_start(x_sb[:, b, 2:TILES, :], x_v[:, b, 2:TILES, :]).then_inc(loaded["x1"], 16)
            sp.dma_start(wo_sb[:], wo.rearrange("(h p) d -> p h d", p=2 * DH)).then_inc(loaded["late"], 16)
            sp.dma_start(we_sb[:], expert_w).then_inc(loaded["late"], 16)
            sp.dma_start(gate_sb[:], gate).then_inc(loaded["late"], 16)
            sp.dma_start(eb_sb[:], expert_b).then_inc(loaded["late"], 16)

            def feed(j, hp, b, s):
                if not (isinstance(s, int) and s < 2):
                    sp.wait_ge(q_turned, s - 1)
                sp.dma_start(q_feed[b][:].bitcast(f32).rearrange("p h d -> p (h d)"),
                             q_split[:, j % 2, b].bitcast(f32).rearrange("p n h s d -> p (n h s d)")
                             [:, bass.ds(hp * 4 * DH, 4 * DH)]).then_inc(q_fed[b], 16)

            def store(t):
                for b in range(B):
                    sp.wait_ge(out_ready, B * t + b + 1)
                    sp.dma_start(out[b, t * T:(t + 1) * T, :], out_sb[b][:]).then_inc(stored, 16)

            for j in range(TILES):
                if j == 0:
                    sp.wait_ge(wide_ready, 2)
                else:
                    sp.wait_ge(q_ready, (j - 1) * STEPS + 2)
                for b in range(B):
                    feed(j, 0, b, j * STEPS + b)
                if j >= 1:
                    sp.wait_ge(q_ready, (j - 1) * STEPS + PAIRS)
                with sp.Fori(1, PAIRS // 2) as hp:
                    for b in range(B):
                        feed(j, hp, b, hp * 2 + (j * STEPS + b))
                if j == 0:
                    sp.wait_ge(wide_ready, 4)
                else:
                    sp.wait_ge(q_ready, j * STEPS)
                if j >= 3:
                    store(j - 3)
                with sp.Fori(PAIRS // 2, PAIRS) as hp:
                    for b in range(B):
                        feed(j, hp, b, hp * 2 + (j * STEPS + b))
            for t in range(TILES - 3, TILES):
                store(t)
            sp.wait_ge(stored, 16 * B * TILES)

        @block.tensor
        def _(pe):
            def fill(free, count):
                pe.wait_ge(free, count)

            def queries(s, b):
                pe.wait_ge(q_fed[b], s * 8 + (16 - 8 * b))
                if not (isinstance(s, int) and s < 1):
                    pe.wait_ge(qT_ready, s)
                turned = q_ps[:].bitcast(f32r)
                nc.tensor.transpose(turned[:, 0:T], q_feed[b][:, 0, :], ident_r[:])
                nc.tensor.transpose(turned[:, T:2 * T], q_feed[b][:, 1, :], ident_r[:]).then_inc(q_turned, 1)

            def qk(j, s, b, h):
                if h == 0:
                    pe.wait_ge(qT_ready, s + 1)
                if not (isinstance(s, int) and s < 1):
                    pe.wait_ge(probs[h], s)
                width = blocks(j) * T
                at, pieces = score_chunks(j)
                for c0, c1 in pieces:
                    nc.tensor.matmul(S[h][:, at + c0:at + c1], qT[b][:, h, :], k_stack[:, 0, b, c0:c1],
                                     start=True, stop=False)
                    nc.tensor.matmul(S[h][:, at + c0:at + c1], qT[b][:, h, :], k_stack[:, 1, b, c0:c1],
                                     start=False, stop=(c1 < width))
                nc.tensor.matmul(S[h][:, at + width - T:at + width], ident_bf[:], mask_bf[:],
                                 start=False, stop=True).then_inc(scores[h], 1)

            def turn_probs(j, s, step, h):
                a, b = bank_counts(j, step)
                pe.wait_ge(probs[h], s + 1)
                nb = blocks(j)
                if uses(j) == 1:
                    chunks = [((bankA, bankB)[h], (fullA, fullB)[h], (freeA, freeB)[h], (a, b)[h], 0, nb)]
                else:
                    chunks = [(bankA, fullA, freeA, a + h, 0, 4), (bankB, fullB, freeB, b + h, 4, nb)]
                for bank_, full, free, count, k0, k1 in chunks:
                    fill(free, count)
                    for k in range(k0, k1):
                        last = nc.tensor.transpose(bank_[:, (k - k0) * T:(k - k0 + 1) * T],
                                                   P[h][:, k * T:(k + 1) * T], ident_sb[:])
                    last.then_inc(full, 1)

            def side_work(j, s, hp, b, last_in_bank):
                if not (isinstance(s, int) and s < 1):
                    if isinstance(s, int) and s == 1:
                        pe.wait_ge(rope_parts, 1)
                    else:
                        pe.wait_ge(o_free, s - 1)
                if j + 1 < TILES:
                    ins = nc.tensor.matmul(o_query, h1T[:, (j + 1) % 2, b, :], wq_sb[:, bass.ds(hp * 2 * DH, 2 * DH)],
                                           start=True, stop=True)
                    if last_in_bank:
                        ins.then_inc(o_full, 1)
                if j >= 2:
                    nc.tensor.matmul(o_expert, h2T[:, j % 2, b, :], we_sb[:, bass.ds(hp * DIM, DIM)],
                                     start=True, stop=True)

            def pv(j, step, b):
                a_count, b_count = bank_counts(j, step)
                pe.wait_ge(freeA, a_count + uses(j))
                pe.wait_ge(freeB, b_count + uses(j))
                nb = blocks(j)
                for k in range(nb):
                    for h in range(2):
                        last = nc.tensor.matmul(o_out[h * DH:(h + 1) * DH, :], v_sb[:, b, k, :],
                                                PT[b][h][:, k * T:(k + 1) * T],
                                                start=(k == 0), stop=(k == nb - 1))
                last.then_inc(o_full, 1)

            def stage(name, t):
                a, b = AT_STAGE[name, t]
                if name == "norm1_T":
                    pe.wait_ge(normed1_ready, t + 1)
                    fill(freeA, a)
                    for i in range(B):
                        last = nc.tensor.transpose(bankA[:, i * T:(i + 1) * T], normed1[:, i, :], ident_sb[:])
                    last.then_inc(fullA, 1)
                elif name == "kv":
                    pe.wait_ge(freeA, AT_STAGE["norm1_T", t][0] + 1)
                    fill(freeB, b)
                    for i in range(B):
                        last = nc.tensor.matmul(bankB[:, i * 2 * DH:(i + 1) * 2 * DH], h1T[:, t % 2, i, :], wkv_sb[:],
                                                start=True, stop=True)
                    last.then_inc(fullB, 1)
                elif name in ("q_first", "q_second"):
                    c = int(name == "q_second")
                    for i, (bank_, full, free, count) in enumerate(((bankA, fullA, freeA, a), (bankB, fullB, freeB, b))):
                        fill(free, count)
                        nc.tensor.matmul(bank_[:], h1T[:, 0, i, :], wq_sb[:, c * BANK:(c + 1) * BANK],
                                         start=True, stop=True).then_inc(full, 1)
                elif name == "k_T":
                    pe.wait_ge(k_ready, t + 1)
                    fill(freeA, a)
                    for k in range(2):
                        for i in range(B):
                            last = nc.tensor.transpose(
                                bankA[:, (2 * k + i) * T:(2 * k + i + 1) * T].bitcast(f32r),
                                k_split[:, i, k:k + 2, :].rearrange("p s d -> p (s d)"), ident_r[:])
                    last.then_inc(fullA, 1)
                elif name == "recip_T":
                    pe.wait_ge(rows_ready, t + 1)
                    for i in range(B):
                        for half, (bank_, full, free, count) in enumerate(
                                ((bankA, fullA, freeA, a + i), (bankB, fullB, freeB, b + i))):
                            fill(free, count)
                            for k in range(4):
                                c = (4 * half + k) * T
                                last = nc.tensor.transpose(bank_[:, k * T:(k + 1) * T],
                                                           recip_rows[:, i, c:c + T], ident_sb[:])
                            last.then_inc(full, 1)
                elif name == "wo":
                    ra, rb = AT_STAGE["recip_T", t]
                    pe.wait_ge(freeA, ra + 2)
                    pe.wait_ge(freeB, rb + 2)
                    fill(freeA, a)
                    for i in range(B):
                        for hp in range(PAIRS):
                            last = nc.tensor.matmul(bankA[:, i * DIM:(i + 1) * DIM], oT_n[:, i, hp, :],
                                                    wo_sb[:, hp, :], start=(hp == 0), stop=(hp == PAIRS - 1))
                    last.then_inc(fullA, 1)
                elif name == "norm2_T":
                    pe.wait_ge(normed2_ready, t + 1)
                    fill(freeB, b)
                    for i in range(B):
                        last = nc.tensor.transpose(bankB[:, i * T:(i + 1) * T], normed2[:, i, :], ident_sb[:])
                    last.then_inc(fullB, 1)
                elif name == "router":
                    nb_ = AT_STAGE["norm2_T", t][1]
                    pe.wait_ge(freeB, nb_ + 1)
                    fill(freeA, a)
                    for i in range(B):
                        last = nc.tensor.matmul(bankA[:, i * EXPERTS:(i + 1) * EXPERTS], h2T[:, t % 2, i, :], gate_sb[:],
                                                start=True, stop=True)
                    last.then_inc(fullA, 1)
                elif name == "comb_T":
                    pe.wait_ge(comb_ready, t + 1)
                    fill(freeB, b)
                    for i in range(B):
                        last = nc.tensor.transpose(bankB[0:EXPERTS, i * T:(i + 1) * T], comb[:, i, :], ident_sb[:])
                    last.then_inc(fullB, 1)
                elif name == "bias":
                    pe.wait_ge(freeB, AT_STAGE["comb_T", t][1] + 1)
                    fill(freeA, a)
                    for i in range(B):
                        last = nc.tensor.matmul(bankA[:, i * DIM:(i + 1) * DIM], combT[:, i, :], eb_sb[:],
                                                start=True, stop=True)
                    last.then_inc(fullA, 1)
                elif name in ("ffn0", "ffn1"):
                    i = int(name[3])
                    for bank_, full, free, count, c in ((bankA, fullA, freeA, a, 0), (bankB, fullB, freeB, b, 1)):
                        fill(free, count)
                        nc.tensor.matmul(bank_[:], h2T[:, t % 2, i, :], we_sb[:, c * BANK:(c + 1) * BANK],
                                         start=True, stop=True).then_inc(full, 1)

            def one_step(j, step, at, hp, b, prev, nxt):
                s = step + j * STEPS
                if not (isinstance(s, int) and s + 2 >= TOTAL):
                    queries(s + 2, b)
                for h in range(2):
                    if nxt is not None:
                        qk(nxt, s + 1, 1 - b, h)
                    turn_probs(j, s, at, h)
                side_work(j, s, hp, b, prev is None)
                if prev is not None:
                    pv(*prev, 1 - b)

            pe.wait_ge(silu_ready, 1)
            for n, m in enumerate((SA, CA, SB, CB)):
                last = nc.tensor.matmul(bankA[:, n * B:(n + 1) * B], wmod_sb[:, m * DIM:(m + 1) * DIM],
                                        silu[:, 2, :], start=True, stop=True)
            last.then_inc(fullA, 1)
            for n, m in enumerate((GA, GB)):
                for i in range(B):
                    last = nc.tensor.matmul(bankB[:, (n * B + i) * DIM:(n * B + i + 1) * DIM], silu_rows[:, i, :],
                                            wmod_sb[:, m * DIM:(m + 1) * DIM], start=True, stop=True)
            last.then_inc(fullB, 1)
            pe.wait_ge(loaded["consts"], 32)
            pe.wait_ge(loaded["w"], 32)
            for name, t in HEAD:
                stage(name, t)
            queries(0, 0)
            queries(1, 1)
            ka, kb = AT_STAGE["k_T", 0]
            pe.wait_ge(freeA, ka + 1)
            pe.wait_ge(masks_ready, 1)
            for h in range(2):
                qk(0, 0, 0, h)
            for j in range(TILES):
                for step in plan(j):
                    if isinstance(step, tuple):
                        with pe.Fori(step[0] // 2, step[1] // 2) as hp:
                            for b in range(B):
                                at = hp * 2 + b
                                one_step(j, at, (at, step[0]), hp, b, (j, (at - 1, step[0])), j)
                        continue
                    prev = (j, step - 1) if step else ((j - 1, STEPS - 1) if j else None)
                    nxt = j if step < STEPS - 1 else (j + 1 if j + 1 < TILES else None)
                    if step == STEPS - 1 and nxt is not None:
                        pe.wait_ge(freeA, AT_STAGE["k_T", nxt][0] + 1)
                    one_step(j, step, step, step // 2, step % 2, prev, nxt)
                    if step == 0 and j == 1:
                        pe.wait_ge(loaded["late"], 64)
                    for name, t in stages(j, step):
                        stage(name, t)
            pe.wait_ge(o_free, TOTAL - 1)
            pv(TILES - 1, STEPS - 1, 1)
            for name, t in TAIL:
                stage(name, t)

        @block.scalar
        def _(act):
            act.dma_start(c_sb[:], c_t).then_inc(loaded["mod"], 16)
            act.dma_start(wmod_sb[:], wmod).then_inc(loaded["mod"], 16)
            act.dma_start(mask_sb[:], mask).then_inc(loaded["consts"], 16)
            act.dma_start(cosk_sb[:], cos_k.rearrange("(j p) d -> p j d", p=T)).then_inc(loaded["tables"], 16)
            act.dma_start(sink_sb[:], sin_k.rearrange("(j p) d -> p j d", p=T)).then_inc(loaded["tables"], 16)

            def turn_queries(s, b):
                act.wait_ge(q_turned, s + 1)
                nc.scalar.copy(qT[b][:].rearrange("p h t -> p (h t)"), q_ps[:, 0:2 * T]).then_inc(qT_ready, 1)

            def keep_probs(j, s, at, b, h):
                a, _ = bank_counts(j, at)
                if uses(j) == 1 and h == 1:
                    return
                cols = min(blocks(j), 4) * T
                act.wait_ge(fullA, a + (h + 1))
                if not (isinstance(s, int) and s < 2):
                    act.wait_ge(o_full, s)
                nc.scalar.copy(PT[b][h][:, 0:cols], bankA[:, 0:cols]).then_inc(freeA, 1)

            def exponential(j, s, hp, b, h, turned):
                act.wait_ge(least_ready[h], s + 1)
                if turned is not None:
                    act.wait_ge(*turned)
                width, at = blocks(j) * T, score_chunks(j)[0]
                nc.scalar.activation(P[h][:, 0:width], S[h][:, at:at + width], ACT.Exp,
                                     bias=least[:, h:h + 1], scale=-1.0,
                                     accum_out=sums[j % 2][:].rearrange("p b h -> p (b h)")
                                     [:, bass.ds(hp * 2 + (b * HEADS + h), 1)]).then_inc(probs[h], 1)

            def one_step(j, step, at, b, nxt, nxt_hp):
                s = step + j * STEPS
                if not (isinstance(s, int) and s + 2 >= TOTAL):
                    turn_queries(s + 2, b)
                a, bb = bank_counts(j, at)
                for h in range(2):
                    keep_probs(j, s, at, b, h)
                    if nxt is not None:
                        if uses(j) == 1:
                            turned = ((fullA, a + 1), (fullB, bb + 1))[h]
                        else:
                            turned = (fullB, bb + (h + 1))
                        exponential(nxt, s + 1, nxt_hp, 1 - b, h, turned)

            def stage(name, t):
                a, b = AT_STAGE[name, t]
                if name == "norm1_T":
                    act.wait_ge(fullA, a + 1)
                    if t == 0:
                        act.wait_ge(freeA, 1)
                    for i in range(B):
                        last = nc.scalar.activation(h1T[:, t % 2, i, :], bankA[:, i * T:(i + 1) * T], ACT.Identity,
                                                    bias=mod_cols[:, 0, i:i + 1], scale=mod_cols[:, 1, i:i + 1])
                    last.then_inc(freeA, 1)
                elif name == "norm2_T":
                    act.wait_ge(fullB, b + 1)
                    for i in range(B):
                        last = nc.scalar.activation(h2T[:, t % 2, i, :], bankB[:, i * T:(i + 1) * T], ACT.Identity,
                                                    bias=mod_cols[:, 2, i:i + 1], scale=mod_cols[:, 3, i:i + 1])
                    last.then_inc(freeB, 1)
                elif name in ("q_first", "q_second"):
                    c = int(name == "q_second")
                    for i in range(B):
                        act.wait_ge(wide_sum, 2 * c + i + 1)
                        nc.scalar.copy(q_split[:, 0, i, 4 * c:4 * c + 4, :, 0, :].rearrange("p n h d -> p (n h) d"),
                                       wide_cos[:, i]).then_inc(wide_high, 1)
                elif name == "k_T":
                    act.wait_ge(fullA, a + 1)
                    nc.scalar.copy(k_stack[:, :, :, t * T:(t + 1) * T],
                                   bankA[:].rearrange("p (s b t) -> p s b t", s=2, b=B)).then_inc(freeA, 1)
                elif name == "router":
                    act.wait_ge(sorted_ready, t + 1)
                    for i in range(B):
                        last = nc.scalar.activation(e_sorted[:, i, :], sorted_l[:, i, :], ACT.Exp,
                                                    bias=neg_top[:, i:i + 1], accum_out=e_sum[:, i:i + 1])
                    last.then_inc(router_exp, 1)

            act.wait_ge(loaded["mod"], 32)
            nc.scalar.activation(silu[:, 0, :], c_sb[:], ACT.Exp, scale=-1.0).then_inc(silu_exp, 1)
            act.wait_ge(loaded["consts"], 32)
            nc.scalar.copy(ident_bf[:], ident_sb[:])
            nc.scalar.copy(ident_r[:], ident_sb[:])
            nc.scalar.copy(mask_bf[:], mask_sb[:]).then_inc(masks_ready, 1)
            for name, t in HEAD:
                stage(name, t)
            turn_queries(0, 0)
            turn_queries(1, 1)
            for h in range(2):
                exponential(0, 0, 0, 0, h, None)
            for j in range(TILES):
                for step in plan(j):
                    if isinstance(step, tuple):
                        with act.Fori(step[0] // 2, step[1] // 2) as hp:
                            for b in range(B):
                                one_step(j, hp * 2 + b, (hp * 2 + b, step[0]), b, j, hp + b)
                        continue
                    nxt = j if step < STEPS - 1 else (j + 1 if j + 1 < TILES else None)
                    one_step(j, step, step, step % 2, nxt, (step + 1) // 2 % PAIRS)
                    for name, t in stages(j, step):
                        stage(name, t)
            for name, t in TAIL:
                stage(name, t)

        @block.vector
        def _(dve):
            links = [0]

            def link(ins):
                links[0] += 1
                ins.then_inc(dve_link, 1)
                dve.wait_ge(dve_link, links[0])

            def smallest(j, s, h):
                dve.wait_ge(scores[h], s + 1)
                width, at = blocks(j) * T, score_chunks(j)[0]
                nc.vector.tensor_reduce(least[:, h:h + 1], S[h][:, at:at + width], AX.X, ALU.min)\
                    .then_inc(least_ready[h], 1)

            def keep_probs(j, s, at, b, h):
                _, bc = bank_counts(j, at)
                if uses(j) == 1 and h == 0:
                    return
                first = 0 if uses(j) == 1 else 4
                cols = (blocks(j) - first) * T
                dve.wait_ge(fullB, bc + 1 if uses(j) == 1 else bc + (h + 1))
                if not (isinstance(s, int) and s < 2):
                    dve.wait_ge(o_full, s)
                nc.vector.tensor_copy(PT[b][h][:, first * T:first * T + cols], bankB[:, 0:cols]).then_inc(freeB, 1)

            def keep_output(j, hp, b):
                nc.vector.tensor_copy(oT[j % 2][:, b].rearrange("p h t -> p (h t)")[:, bass.ds(hp * T, T)],
                                      o_out).then_inc(o_free, 1)

            def expert(j, step, hp, b):
                weight = comb[:, b, bass.ds(hp, 1)]
                if isinstance(step, int) and step < 2:
                    ins = nc.vector.tensor_scalar(y[b][:], o_expert, weight, None, ALU.mult)
                else:
                    dve.wait_ge(y_added, step + ((j - 2) * STEPS - 1))
                    ins = nc.vector.scalar_tensor_tensor(out=y[b][:], in0=o_expert, scalar=weight, in1=y[b][:],
                                                         op0=ALU.mult, op1=ALU.add)
                ins.then_inc(y_added, 1)

            def one_step(j, step, at, hp, b, nxt, prev, prev_hp):
                s = step + j * STEPS
                for h in range(2):
                    if nxt is not None:
                        smallest(nxt, s + 1, h)
                    keep_probs(j, s, at, b, h)
                if isinstance(step, int) and step == 0 and j >= 2:
                    combine_weights(j - 2)
                dve.wait_ge(o_full, s + 1)
                if j + 1 < TILES:
                    if not (isinstance(s, int) and s < 2):
                        dve.wait_ge(q_ready, s - 1)
                    rope(o_query, rope_cos[:, b], rope_sin[:, b], cosq_sb[:, j + 1, :], sinq_sb[:, j + 1, :], 2)\
                        .then_inc(rope_parts, 1)
                if j >= 2:
                    expert(j, step, hp, b)
                if prev is not None:
                    keep_output(prev, prev_hp, 1 - b)

            def norm_stats(tiles, stats_, mean_var_):
                for i in range(B):
                    last = nc.vector.bn_stats(stats_[:, i, :], tiles[:, i, :])
                link(last)
                for i in range(B):
                    last = nc.vector.bn_aggr(mean_var_[:, i, :], stats_[:, i, :])
                last.then_inc(stats_ready, 1)

            def normalise(tiles, dst, mean_var_, rstd_, ready):
                for i in range(B):
                    last = nc.vector.tensor_scalar(dst[:, i, :], tiles[:, i, :], mean_var_[:, i, 0:1],
                                                   rstd_[:, i:i + 1], ALU.subtract, ALU.mult)
                last.then_inc(ready, 1)

            def norm1_stats(t):
                if t < TILES:
                    norm_stats(x_sb[:, :, t, :], stats, mean_var)

            def norm1(t):
                if t < TILES:
                    dve.wait_ge(rstd_ready, RSTD[1, t])
                    if t >= 1:
                        dve.wait_ge(fullA, AT_STAGE["norm1_T", t - 1][0] + 1)
                    normalise(x_sb[:, :, t, :], normed1, mean_var, rstd, normed1_ready)

            def norm2_stats(t):
                dve.wait_ge(x1_ready, t + 1)
                norm_stats(x_sb[:, :, t, :], stats2, mean_var2)

            def norm2(t):
                dve.wait_ge(rstd_ready, RSTD[2, t])
                normalise(x_sb[:, :, t, :], normed2, mean_var2, rstd2, normed2_ready)

            def rope(columns, dst_cos, dst_sin, cos, sin, heads):
                nc.vector.tensor_tensor(dst_cos, columns.rearrange("p (h d) -> p h d", d=DH),
                                        cos.unsqueeze(1).to_broadcast([T, heads, DH]), ALU.mult)
                return nc.vector.tensor_tensor(
                    dst_sin.rearrange("p h (x d) -> p h x d", x=2), halves_swapped(columns),
                    sin.rearrange("p (x d) -> p x d", x=2).unsqueeze(1).to_broadcast([T, heads, 2, HALF]), ALU.mult)

            def stage(name, t):
                a, b = AT_STAGE[name, t]
                if name == "kv":
                    dve.wait_ge(fullB, b + 1)
                    kv = bankB[:, 0:B * 2 * DH].rearrange("p (b d) -> p b d", b=B)
                    nc.vector.tensor_copy(v_sb[:, :, t, :], kv[:, :, DH:2 * DH])
                    if t >= 1:
                        dve.wait_ge(k_ready, t)
                    for i in range(B):
                        last = rope(bankB[:, i * 2 * DH:i * 2 * DH + DH], k_cos[:, i:i + 1], k_sin[:, i:i + 1],
                                    cosk_sb[:, t, :], sink_sb[:, t, :], 1)
                    last.then_inc(freeB, 1)
                elif name in ("q_first", "q_second"):
                    c = int(name == "q_second")

                    def low(i):
                        dve.wait_ge(wide_high, 2 * c + i + 1)
                        heads = q_split[:, 0, i, 4 * c:4 * c + 4]
                        nc.vector.tensor_tensor(heads[:, :, :, 1, :].rearrange("p n h d -> p (n h) d"), wide_cos[:, i],
                                                heads[:, :, :, 0, :].rearrange("p n h d -> p (n h) d").bitcast(f32),
                                                ALU.subtract).then_inc(wide_ready, 1)

                    for i, (bank_, full, free, count) in enumerate(((bankA, fullA, freeA, a), (bankB, fullB, freeB, b))):
                        dve.wait_ge(full, count + 1)
                        if c == 1:
                            dve.wait_ge(wide_ready, i + 1)
                        rope(bank_[:], wide_cos[:, i], wide_sin[:, i], cosq_sb[:, 0, :], sinq_sb[:, 0, :], 8)\
                            .then_inc(free, 1)
                    for i in range(B):
                        low(i)
                elif name == "recip_T":
                    for i in range(B):
                        for half, (bank_, full, free, count) in enumerate(
                                ((bankA, fullA, freeA, a + i), (bankB, fullB, freeB, b + i))):
                            dve.wait_ge(full, count + 1)
                            hs = slice(4 * half, 4 * half + 4)
                            nc.vector.tensor_tensor(oT_n[:, i, hs, :], oT[t % 2][:, i, hs, :],
                                                    bank_[:].rearrange("p (h t) -> p h t", h=4), ALU.mult)\
                                .then_inc(free, 1)
                elif name == "wo":
                    dve.wait_ge(fullA, a + 1)
                    nc.vector.tensor_tensor(attn[:], bankA[:, 0:B * DIM].rearrange("p (b d) -> p b d", b=B),
                                            gates[:, 0], ALU.mult).then_inc(freeA, 1)
                elif name == "router":
                    dve.wait_ge(fullA, a + 1)
                    nc.vector.tensor_copy(logits[:], bankA[:, 0:B * EXPERTS].rearrange("p (b e) -> p b e", b=B))\
                        .then_inc(freeA, 1)
                    dve.wait_ge(freeA, a + 1)
                    for i in range(B):
                        last = nc.vector.max(sorted_l[:, i, :], logits[:, i, :])
                    link(last)
                    nc.vector.tensor_scalar(neg_top[:], sorted_l[:, :, 0], -1.0, None, ALU.mult).then_inc(sorted_ready, 1)
                    for i in range(B):
                        last = nc.vector.max_index(top_idx[:, i, :], sorted_l[:, i, :], logits[:, i, :])
                    link(last)
                    link(nc.vector.tensor_copy(top_idx_f[:], top_idx[:]))
                elif name == "comb_T":
                    dve.wait_ge(fullB, b + 1)
                    nc.vector.tensor_copy(combT[:], bankB[0:EXPERTS, 0:B * T].rearrange("p (b t) -> p b t", b=B))\
                        .then_inc(freeB, 1)
                elif name == "bias":
                    dve.wait_ge(fullA, a + 1)
                    if t < TILES - 2:
                        dve.wait_ge(y_added, t * STEPS + 2)
                        for i in range(B):
                            last = nc.vector.tensor_tensor(y[i][:], y[i][:], bankA[:, i * DIM:(i + 1) * DIM], ALU.add)
                    else:
                        for i in range(B):
                            last = nc.vector.tensor_copy(y[i][:], bankA[:, i * DIM:(i + 1) * DIM])
                    last.then_inc(freeA, 1)
                    dve.wait_ge(freeA, a + 1)
                elif name in ("ffn0", "ffn1"):
                    i = int(name[3])
                    for bank_, full, free, count, c in ((bankA, fullA, freeA, a, 0), (bankB, fullB, freeB, b, 1)):
                        dve.wait_ge(full, count + 1)
                        for e in range(4):
                            ins = nc.vector.scalar_tensor_tensor(
                                out=y[i][:], in0=bank_[:, e * DIM:(e + 1) * DIM],
                                scalar=comb[:, i, 4 * c + e:4 * c + e + 1], in1=y[i][:],
                                op0=ALU.mult, op1=ALU.add)
                            if e == 3:
                                ins.then_inc(free, 1)
                                dve.wait_ge(free, count + 1)
                            else:
                                link(ins)
                    gate_y(t, i)

            def gate_y(t, i):
                if t >= 1:
                    dve.wait_ge(out_ready, B * (t - 1) + i + 1)
                nc.vector.tensor_tensor(y_gated[i][:], y[i][:], gates[:, 1, i, :], ALU.mult).then_inc(y_ready, 1)

            def reciprocals(t):
                dve.wait_ge(probs[0], STEPS * (t + 1))
                dve.wait_ge(probs[1], STEPS * (t + 1))
                nc.vector.reciprocal(recips[:], sums[t % 2][:]).then_inc(recips_ready, 1)
                dve.wait_ge(recips_ready, t + 1)
                if t >= 1:
                    dve.wait_ge(fullB, AT_STAGE["recip_T", t - 1][1] + 2)
                nc.vector.tensor_copy(recip_rows[:].rearrange("p b (h d) -> p (b h) d", d=DH),
                                      recips[:].rearrange("p b h -> p (b h)").unsqueeze(2)
                                      .to_broadcast([T, B * HEADS, DH])).then_inc(rows_ready, 1)

            def combine_weights(t):
                dve.wait_ge(router_exp, t + 1)
                link(nc.vector.reciprocal(e_rec[:], e_sum[:]))
                link(nc.vector.tensor_tensor(top_w[:], e_sorted[:, :, 0:TOPK],
                                             e_rec[:].unsqueeze(2).to_broadcast([T, B, TOPK]), ALU.mult))
                for i in range(B):
                    for k in range(TOPK):
                        last = nc.vector.tensor_scalar(comb_k[:, i, k, :], iota_sb[:], top_idx_f[:, i, k:k + 1],
                                                       top_w[:, i, k:k + 1], ALU.is_equal, ALU.mult)
                link(last)
                if t >= 1:
                    dve.wait_ge(y_ready, B * t)
                    dve.wait_ge(fullB, AT_STAGE["comb_T", t - 1][1] + 1)
                nc.vector.tensor_tensor(comb[:], comb_k[:, :, 0, :], comb_k[:, :, 1, :], ALU.add).then_inc(comb_ready, 1)
                dve.wait_ge(comb_ready, t + 1)

            dve.wait_ge(loaded["x0"], 16 * B)
            norm1_stats(0)
            dve.wait_ge(silu_exp, 1)
            link(nc.vector.tensor_scalar_add(silu[:, 1, :], silu[:, 0, :], 1.0))
            link(nc.vector.reciprocal(silu[:, 0, :], silu[:, 1, :]))
            link(nc.vector.tensor_tensor(silu[:, 2, :], silu[:, 0, :], c_sb[:], ALU.mult))
            nc.vector.tensor_copy(silu_rows[:], silu[:, 2, :].unsqueeze(2).to_broadcast([DIM, B, T])).then_inc(silu_ready, 1)
            norm1(0)
            dve.wait_ge(fullA, 1)
            cols = bankA[:, 0:4 * B].rearrange("p (m b) -> p m b", b=B)
            nc.vector.tensor_copy(mod_cols[:, 0:4:2, :], cols[:, 0:4:2, :])
            nc.vector.tensor_scalar_add(mod_cols[:, 1:4:2, :], cols[:, 1:4:2, :], 1.0).then_inc(freeA, 1)
            dve.wait_ge(fullB, 1)
            nc.vector.tensor_copy(gate_tmp[:, 2, :], bankB[:]).then_inc(freeB, 1)
            dve.wait_ge(loaded["tables"], 64)
            norm1_stats(1)
            for name, t in HEAD:
                if (name, t) == ("norm1_T", 1):
                    norm1(1)
                stage(name, t)
            for h in range(2):
                smallest(0, 0, h)

            def gate_rows():
                g = gate_tmp[:, 2, :]
                link(nc.vector.tensor_scalar(gate_tmp[:, 0, :], g, -1.0, None, ALU.mult))
                link(nc.vector.tensor_tensor(gate_tmp[:, 1, :], g, gate_tmp[:, 0, :], ALU.max))
                nc.vector.tensor_scalar(gate_tmp[:, 1, :], gate_tmp[:, 1, :], 0.25, None, ALU.max)
                link(nc.vector.tensor_scalar(gate_tmp[:, 0, :], g, 0.0, 2.0, ALU.is_ge, ALU.mult))
                link(nc.vector.tensor_scalar(gate_tmp[:, 0, :], gate_tmp[:, 0, :], -1.0, None, ALU.add))
                link(nc.vector.tensor_tensor(gates[:].rearrange("p g b d -> p (g b d)"), gate_tmp[:, 0, :],
                                             gate_tmp[:, 1, :], ALU.mult))

            for j in range(TILES):
                for step in plan(j):
                    if isinstance(step, tuple):
                        with dve.Fori(step[0] // 2, step[1] // 2) as hp:
                            for b in range(B):
                                one_step(j, hp * 2 + b, (hp * 2 + b, step[0]), hp, b, j, j, hp - (1 - b))
                        if step[1] == 14 and j >= 1:
                            norm2(j - 1)
                        continue
                    prev = j if step else (j - 1 if j else None)
                    prev_hp = (step - 1) // 2 if step else PAIRS - 1
                    nxt = j if step < STEPS - 1 else (j + 1 if j + 1 < TILES else None)
                    one_step(j, step, step, step // 2, step % 2, nxt, prev, prev_hp)
                    if step == 0 and j == 0:
                        gate_rows()
                        dve.wait_ge(loaded["x1"], 16 * B)
                        dve.wait_ge(consts_ready, 1)
                    if step == 0 and j >= 1:
                        reciprocals(j - 1)
                    for name, t in stages(j, step):
                        stage(name, t)
                    if step == 0:
                        norm1_stats(j + 2)
                    if step == 1:
                        norm1(j + 2)
                    if step == 9 and j >= 1:
                        norm2_stats(j - 1)
                    if step == STEPS - 1 and j >= 2:
                        dve.wait_ge(y_added, (j - 1) * STEPS)
                        for i in range(B):
                            gate_y(j - 2, i)
            dve.wait_ge(o_full, TOTAL + 1)
            keep_output(TILES - 1, PAIRS - 1, 1)
            reciprocals(TILES - 1)
            for name, t in TAIL:
                if name == "comb_T":
                    combine_weights(t)
                stage(name, t)
                if (name, t) == ("wo", TILES - 1):
                    norm2_stats(TILES - 1)
                    norm2(TILES - 1)

        @block.gpsimd
        def _(pool):
            links = [0]

            def link(ins):
                links[0] += 1
                ins.then_inc(pool_link, 1)
                pool.wait_ge(pool_link, links[0])

            def inverse_deviation(count, mean_var_, var_eps_, rstd_):
                pool.wait_ge(stats_ready, count)
                link(nc.gpsimd.tensor_scalar(var_eps_[:], mean_var_[:, :, 1], EPS, None, ALU.add))
                nc.gpsimd.tensor_tensor(rstd_[:], var_eps_[:], minus_half[:], ALU.pow).then_inc(rstd_ready, 1)

            def keys(t):
                pool.wait_ge(freeB, AT_STAGE["kv", t][1] + 1)
                if t >= 1:
                    pool.wait_ge(fullA, AT_STAGE["k_T", t - 1][0] + 1)
                link(nc.gpsimd.tensor_tensor(k_cos[:], k_cos[:], k_sin[:], ALU.add))
                nc.gpsimd.tensor_copy(k_split[:, :, 2, :], k_cos[:])
                link(nc.gpsimd.tensor_copy(k_split[:, :, 0, :], k_cos[:]))
                nc.gpsimd.tensor_tensor(k_split[:, :, 1, :], k_cos[:], k_split[:, :, 0, :].bitcast(f32),
                                        ALU.subtract).then_inc(k_ready, 1)

            def wide_queries(c):
                for i in range(B):
                    a, b = AT_STAGE[("q_first", "q_second")[c], 0]
                    pool.wait_ge((freeA, freeB)[i], (a, b)[i] + 1)
                    nc.gpsimd.tensor_tensor(wide_cos[:, i], wide_cos[:, i], wide_sin[:, i], ALU.add).then_inc(wide_sum, 1)

            def query_pair(j, step, hp, b):
                n = step + (j * STEPS + 1)
                pool.wait_ge(rope_parts, n)
                nc.gpsimd.tensor_tensor(rope_cos[:, b], rope_cos[:, b], rope_sin[:, b], ALU.add).then_inc(rope_sum, 1)
                pair = q_split[:, (j + 1) % 2, b, bass.ds(hp, 1)]
                pool.wait_ge(rope_sum, n)
                nc.gpsimd.tensor_copy(pair[:, :, :, 0, :], rope_cos[:, b].unsqueeze(1)).then_inc(rope_high, 1)
                pool.wait_ge(rope_high, n)
                nc.gpsimd.tensor_tensor(pair[:, :, :, 1, :], rope_cos[:, b].unsqueeze(1),
                                        pair[:, :, :, 0, :].bitcast(f32), ALU.subtract).then_inc(q_ready, 1)

            def residual(t):
                pool.wait_ge(freeA, AT_STAGE["wo", t][0] + 1)
                nc.gpsimd.tensor_tensor(x_sb[:, :, t, :], x_sb[:, :, t, :], attn[:], ALU.add).then_inc(x1_ready, 1)

            def result(t, i):
                pool.wait_ge(y_ready, B * t + i + 1)
                if t >= 1:
                    pool.wait_ge(stored, 16 * B * t)
                nc.gpsimd.tensor_tensor(out_sb[i][:], y_gated[i][:], x_sb[:, i, t, :], ALU.add).then_inc(out_ready, 1)

            link(nc.gpsimd.memset(minus_half[:], -0.5))
            nc.gpsimd.iota(iota_sb[:], pattern=[[1, EXPERTS]], base=0, channel_multiplier=0,
                           allow_small_or_imprecise_dtypes=True).then_inc(consts_ready, 1)
            inverse_deviation(RSTD[1, 0], mean_var, var_eps, rstd)
            inverse_deviation(RSTD[1, 1], mean_var, var_eps, rstd)
            keys(0)
            wide_queries(0)
            wide_queries(1)
            for j in range(TILES):
                if 1 <= j < TILES - 1:
                    pool.wait_ge(q_turned, j * STEPS)
                for step in plan(j):
                    if isinstance(step, tuple):
                        if j + 1 < TILES:
                            with pool.Fori(step[0] // 2, step[1] // 2) as hp:
                                for b in range(B):
                                    query_pair(j, hp * 2 + b, hp, b)
                        continue
                    if j + 1 < TILES:
                        query_pair(j, step, step // 2, step % 2)
                    if step == 0 and j + 1 < TILES:
                        keys(j + 1)
                    if step == 0 and j + 2 < TILES:
                        inverse_deviation(RSTD[1, j + 2], mean_var, var_eps, rstd)
                    if step == 8 and j >= 1:
                        residual(j - 1)
                    if step == 9 and j >= 1:
                        inverse_deviation(RSTD[2, j - 1], mean_var2, var_eps2, rstd2)
                    if step == STEPS - 1 and j >= 2:
                        for i in range(B):
                            result(j - 2, i)
            residual(TILES - 1)
            inverse_deviation(RSTD[2, TILES - 1], mean_var2, var_eps2, rstd2)
            for t in (TILES - 2, TILES - 1):
                for i in range(B):
                    result(t, i)


def rope_tables():
    inv_freq = (1.0 / np.power(np.float32(10000.0), np.arange(0, DH, 2, dtype=np.float32) / np.float32(DH))).astype(np.float32)
    freqs = np.arange(N, dtype=np.float32)[:, None] * inv_freq[None, :]
    cos = np.cos(np.concatenate([freqs, freqs], axis=1)).astype(np.float32)
    sin = np.sin(np.concatenate([-freqs, freqs], axis=1)).astype(np.float32)
    s = np.float32(-SCALE)
    return cos * s, sin * s, cos, sin


def kernel(L0_attn_x, L0_attn_Wq, L0_attn_Wkv, L0_attn_Wo, L0_ffn_gate_w, L0_ffn_expert_w, L0_ffn_expert_b,
           L0_c, L0_wmod):
    import concourse.bacc as bacc
    from concourse.bass_utils import run_bass_kernel_spmd

    cos_q, sin_q, cos_k, sin_k = rope_tables()
    later = np.arange(T)[None, :] > np.arange(T)[:, None]
    arrays = {
        "x": L0_attn_x, "wq": L0_attn_Wq, "wkv": L0_attn_Wkv, "wo": L0_attn_Wo,
        "gate": np.transpose(L0_ffn_gate_w),
        "expert_w": np.transpose(L0_ffn_expert_w, (2, 0, 1)).reshape(DIM, EXPERTS * DIM),
        "expert_b": L0_ffn_expert_b, "c_t": np.transpose(L0_c), "wmod": L0_wmod,
        "cos_q": cos_q, "sin_q": sin_q, "cos_k": cos_k, "sin_k": sin_k,
        "ident": np.eye(T, dtype=np.float32),
        "mask": np.where(later, np.float32(MASKED), np.float32(0.0)),
    }
    arrays = {k: np.ascontiguousarray(v) for k, v in arrays.items()}
    nc = bacc.Bacc("TRN2", target_bir_lowering=False, num_devices=1)
    aps = [nc.dram_tensor(f"{k}_dram", v.shape, mybir.dt.from_np(v.dtype), kind="ExternalInput").ap()
           for k, v in arrays.items()]
    out = nc.dram_tensor("out_dram", (B, N, DIM), mybir.dt.float32, kind="ExternalOutput").ap()
    build(nc, *aps, out)
    r = run_bass_kernel_spmd(nc, [{f"{k}_dram": v for k, v in arrays.items()}], core_ids=[0])
    return r.results[0]["out_dram"]
```

```python
import numpy as np
import concourse.bass as bass
from concourse import mybir
from contextlib import ExitStack


B, N, DIM = 2, 1024, 128
HEADS, DH = 16, 64
HALF = DH // 2
EXPERTS, TOPK = 8, 2
T = 128
TILES = N // T
PAIRS = HEADS // 2
STEPS = PAIRS * B
TOTAL = TILES * STEPS
BANK = 512
SCALE = float(DH) ** -0.5
EPS = 1e-5
MASKED = 3.0e38
SA, CA, GA, SB, CB, GB = range(6)

LOOPS = ((2, 8), (10, 14))


def blocks(j):
    return j + 1


def uses(j):
    return 1 if blocks(j) <= 4 else 2


def first_part(j):
    return blocks(j) if uses(j) == 1 else min(blocks(j) - 2, 4)


ACT_ALONE = 1
ROWS_BY_VECTOR = 2


def stages(j, step):
    table = {
        0: [("kv", j + 1)],
        1: [("wo", j - 1), ("comb_T", j - 2)],
        9: [("norm2_T", j - 1), ("k_T", j + 1)],
        14: [("norm1_T", j + 2), ("router", j - 1)],
        15: [("bias", j - 2)],
    }
    if j == 0:
        table[0] = [("kv", 1), ("q_second", 0)]
    return [(name, t) for name, t in table.get(step, []) if 0 <= t < TILES]


HEAD = [("norm1_T", 0), ("kv", 0), ("q_first", 0), ("k_T", 0), ("norm1_T", 1)]
TAIL = [("comb_T", TILES - 2), ("bias", TILES - 2), ("norm2_T", TILES - 1), ("router", TILES - 1),
        ("comb_T", TILES - 1)]
FILLS = {"norm1_T": (0, 1), "kv": (0, 1), "q_first": (1, 1), "q_second": (1, 1), "k_T": (1, 0),
         "wo": (1, 0), "norm2_T": (0, 1), "router": (1, 0), "comb_T": (0, 1),
         "bias": (1, 0)}


def ledger():
    a, b = 1, 0
    at_step, at_stage = {}, {}

    def stage(name, t):
        nonlocal a, b
        at_stage[name, t] = (a, b)
        a, b = a + FILLS[name][0], b + FILLS[name][1]

    for name, t in HEAD:
        stage(name, t)
    for j in range(TILES):
        for step in range(STEPS):
            at_step[j, step] = (a, b)
            a, b = a + uses(j), b + uses(j)
            for name, t in stages(j, step):
                stage(name, t)
    for name, t in TAIL:
        stage(name, t)
    return at_step, at_stage


AT_STEP, AT_STAGE = ledger()

RSTD = {(1, 0): 1, (1, 1): 2}
for _j in range(TILES):
    if _j >= 1:
        RSTD[2, _j - 1] = len(RSTD) + 1
    if _j + 2 < TILES:
        RSTD[1, _j + 2] = len(RSTD) + 1
RSTD[2, TILES - 1] = len(RSTD) + 1


def added(t, n):
    return n + (t * (STEPS + B) + B)


def summed_before(t, expert, b):
    return ((t - (TILES - 2)) * EXPERTS + expert) * B + b


def bank_counts(j, step):
    if isinstance(step, tuple):
        step, first = step
        a, b = AT_STEP[j, first]
        return (step - first) * uses(j) + a, (step - first) * uses(j) + b
    return AT_STEP[j, step]


def plan(j):
    steps, at = [], 0
    for first, end in LOOPS:
        steps += list(range(at, first)) + [(first, end)]
        at = end
    return steps + list(range(at, STEPS))


def score_chunks(j):
    width = blocks(j) * T
    if width % BANK == T and width > BANK:
        return T, [(0, BANK - T), (BANK - T, width)]
    return 0, [(c, min(c + BANK, width)) for c in range(0, width, BANK)]


def build(nc, x, wq, wkv, wo, gate, expert_w, expert_b, c_t, wmod,
          cos_q, sin_q, cos_k, sin_k, ident, mask, out):
    f32, f32r, bf16, u32 = mybir.dt.float32, mybir.dt.float32r, mybir.dt.bfloat16, mybir.dt.uint32
    ALU, ACT, AX = mybir.AluOpType, mybir.ActivationFunctionType, mybir.AxisListType

    ctx = ExitStack()
    with ctx:
        def sb(name, shape, dt=f32):
            return ctx.enter_context(nc.sbuf_tensor(name, shape, dt))

        def bank(name, shape):
            return ctx.enter_context(nc.psum_tensor(name, shape, f32))

        def sem(name):
            return ctx.enter_context(nc.semaphore(name))

        x_sb = sb("x_sb", [T, B, TILES, DIM])
        wq_sb = sb("wq_sb", [DIM, HEADS * DH])
        wkv_sb = sb("wkv_sb", [DIM, 2 * DH])
        wo_sb = sb("wo_sb", [2 * DH, PAIRS, DIM])
        we_sb = sb("we_sb", [DIM, EXPERTS * DIM])
        gate_sb = sb("gate_sb", [DIM, EXPERTS])
        eb_sb = sb("eb_sb", [EXPERTS, DIM])
        wmod_sb = sb("wmod_sb", [DIM, 6 * DIM])
        c_sb = sb("c_sb", [DIM, B])
        cosq_sb, sinq_sb, cosk_sb, sink_sb = (sb(n, [T, TILES, DH]) for n in ("cosq", "sinq", "cosk", "sink"))
        ident_sb = sb("ident_sb", [T, T])
        mask_sb = sb("mask_sb", [T, T])
        ident_r = sb("ident_r", [T, T], f32r)
        ident_bf = sb("ident_bf", [T, T], bf16)
        mask_bf = sb("mask_bf", [T, T], bf16)
        minus_half = sb("minus_half", [T, B])
        unused = sb("unused", [T, B])
        ones = sb("ones", [T, 2, DH])
        iota_sb = sb("iota_sb", [T, EXPERTS])
        silu = sb("silu", [DIM, 3, B])
        silu_rows = sb("silu_rows", [DIM, B, T])
        mod_cols = sb("mod_cols", [DIM, 4, B])
        gates = sb("gates", [T, 2, B, DIM])
        gate_tmp = sb("gate_tmp", [T, 3, 2 * B * DIM])
        stats = sb("stats", [T, B, 6])
        mean_var = sb("mean_var", [T, B, 2])
        var_eps = sb("var_eps", [T, B])
        rstd = sb("rstd", [T, B])
        normed1 = sb("normed1", [T, B, DIM])
        stats2 = sb("stats2", [T, B, 6])
        mean_var2 = sb("mean_var2", [T, B, 2])
        var_eps2 = sb("var_eps2", [T, B])
        rstd2 = sb("rstd2", [T, B])
        normed2 = sb("normed2", [T, B, DIM])
        h1T = sb("h1T", [DIM, 2, B, T])
        h2T = sb("h2T", [DIM, 2, B, T])
        k_split = sb("k_split", [T, B, 3, DH], f32r)
        k_cos = sb("k_cos", [T, B, DH])
        k_sin = sb("k_sin", [T, B, DH])
        k_stack = sb("k_stack", [2 * DH, 2, B, N], f32r)
        v_sb = sb("v_sb", [T, B, TILES, DH])
        rope_cos = sb("rope_cos", [T, B, 2, DH])
        rope_sin = sb("rope_sin", [T, B, 2, DH])
        wide_cos = sb("wide_cos", [T, 2, HEADS // 2, DH])
        wide_sin = sb("wide_sin", [T, 2, HEADS // 2, DH])
        q_split = sb("q_split", [T, 2, B, PAIRS, 2, 2, DH], f32r)
        q_feed = [sb(f"q_feed{i}", [T, 2, 2 * DH], f32r) for i in range(2)]
        qT = [sb(f"qT{i}", [2 * DH, 2, T], f32r) for i in range(2)]
        least = sb("least", [T, 2])
        P = [sb(f"P{i}", [T, N]) for i in range(2)]
        PT = [[sb(f"PT{i}{h}", [T, N]) for h in range(2)] for i in range(2)]
        sums = [sb(f"sums{i}", [T, 2]) for i in range(B)]
        recips = [sb(f"recips{i}", [T, 2]) for i in range(B)]
        recip_rows = [sb(f"recip_rows{i}", [T, 2, DH]) for i in range(B)]
        recip_cols = [sb(f"recip_cols{i}", [2 * DH, T]) for i in range(B)]
        oT = [sb(f"oT{i}", [2 * DH, B, PAIRS, T]) for i in range(2)]
        attn = sb("attn", [T, B, DIM])
        logits = sb("logits", [T, B, EXPERTS])
        sorted_l = sb("sorted_l", [T, B, 8])
        neg_top = sb("neg_top", [T, B])
        e_sorted = sb("e_sorted", [T, B, 8])
        e_sum = sb("e_sum", [T, B])
        e_rec = sb("e_rec", [T, B])
        top_idx = sb("top_idx", [T, B, 8], u32)
        top_idx_f = sb("top_idx_f", [T, B, 8])
        top_w = sb("top_w", [T, B, TOPK])
        comb_k = sb("comb_k", [T, B, TOPK, EXPERTS])
        comb = [sb(f"comb{i}", [T, B, EXPERTS]) for i in range(2)]
        combT = sb("combT", [EXPERTS, B, T])
        y = [sb(f"y{b}", [T, DIM]) for b in range(B)]
        y_last = [sb(f"y_last{b}", [T, DIM]) for b in range(B)]
        scaled = sb("scaled", [T, B, 4, DIM])
        y_gated = [sb(f"y_gated{b}", [T, DIM]) for b in range(B)]
        out_sb = [sb(f"out_sb{b}", [T, DIM]) for b in range(B)]

        S = [bank(f"S{h}", [T, N]) for h in range(2)]
        bankA = bank("bankA", [T, BANK])
        bankB = bank("bankB", [T, BANK])
        o_ps = bank("o_ps", [T, BANK])
        q_ps = bank("q_ps", [T, BANK])
        o_out, o_query, o_expert = (o_ps[:, i * T:(i + 1) * T] for i in range(3))

        def last_bank(t, half, b):
            if t == TILES - 1:
                return S[b][:, half * BANK:(half + 1) * BANK]
            return (S[half][:, BANK:2 * BANK], (o_ps, q_ps)[half][:])[b]

        def halves_swapped(columns):
            (pitch, parts), (_, n) = columns.ap
            return bass.AP(tensor=columns.tensor, offset=columns.offset + HALF,
                           ap=[[pitch, parts], [DH, n // DH], [-HALF, 2], [1, HALF]])

        loaded = {n: sem(f"loaded_{n}") for n in ("x0", "x1", "c", "mod", "tables0", "tables", "consts", "mask", "wkv", "wq", "late")}
        gates_full = sem("gates_full")
        gates_read = sem("gates_read")
        masks_ready = sem("masks_ready")
        halves_ready = sem("halves_ready")
        consts_ready = sem("consts_ready")
        silu_exp = sem("silu_exp")
        silu_ready = sem("silu_ready")
        stats_ready = sem("stats_ready")
        rstd_ready = sem("rstd_ready")
        normed1_ready = sem("normed1_ready")
        normed2_ready = sem("normed2_ready")
        fullA, fullB = sem("fullA"), sem("fullB")
        freeA, freeB = sem("freeA"), sem("freeB")
        k_parts = sem("k_parts")
        k_ready = sem("k_ready")
        wide_parts, wide_sum, wide_high = sem("wide_parts"), sem("wide_sum"), sem("wide_high")
        wide_ready = sem("wide_ready")
        rope_parts = sem("rope_parts")
        rope_sum = sem("rope_sum")
        rope_high = sem("rope_high")
        q_ready = sem("q_ready")
        q_fed = [sem(f"q_fed{i}") for i in range(2)]
        q_turned = sem("q_turned")
        qT_ready = sem("qT_ready")
        scores = [sem("scores_even"), sem("scores_odd")]
        least_ready = [sem("least_even"), sem("least_odd")]
        probs = [sem("probs_even"), sem("probs_odd")]
        o_full = sem("o_full")
        o_free = sem("o_free")
        recips_ready = sem("recips_ready")
        rows_ready = sem("rows_ready")
        cols_ready = sem("cols_ready")
        wo_last = sem("wo_last")
        attn_last = sem("attn_last")
        x1_last = sem("x1_last")
        products = sem("products")
        summed = sem("summed")
        scaled_ready = sem("scaled_ready")
        rest_summed = sem("rest_summed")
        finishing = sem("finishing")
        out_last = sem("out_last")
        x1_ready = sem("x1_ready")
        sorted_ready = sem("sorted_ready")
        router_exp = sem("router_exp")
        comb_ready = sem("comb_ready")
        y_added = sem("y_added")
        y_ready = sem("y_ready")
        out_ready = sem("out_ready")
        stored = sem("stored")
        dve_link, pool_link = sem("dve_link"), sem("pool_link")

        block = ctx.enter_context(nc.Block())

        @block.sync
        def _(sp):
            x_v = x.rearrange("b (j p) d -> p b j d", p=T)
            for b in range(B):
                sp.dma_start(x_sb[:, b, 0:2, :], x_v[:, b, 0:2, :]).then_inc(loaded["x0"], 16)
            sp.dma_start(wmod_sb[:], wmod).then_inc(loaded["mod"], 16)
            sp.dma_start(ident_sb[:], ident).then_inc(loaded["consts"], 16)
            sp.dma_start(wkv_sb[:], wkv).then_inc(loaded["wkv"], 16)
            tables = [(dst, src.rearrange("(j p) d -> p j d", p=T)) for dst, src in
                      ((cosk_sb, cos_k), (sink_sb, sin_k), (cosq_sb, cos_q), (sinq_sb, sin_q))]
            for dst, src in tables:
                sp.dma_start(dst[:, 0:1, :], src[:, 0:1, :]).then_inc(loaded["tables0"], 16)
            sp.dma_start(wq_sb[:], wq).then_inc(loaded["wq"], 16)
            sp.dma_start(mask_sb[:], mask).then_inc(loaded["mask"], 16)
            for dst, src in tables:
                sp.dma_start(dst[:, 1:TILES, :], src[:, 1:TILES, :]).then_inc(loaded["tables"], 16)
            for b in range(B):
                sp.dma_start(x_sb[:, b, 2:TILES, :], x_v[:, b, 2:TILES, :]).then_inc(loaded["x1"], 16)
            sp.dma_start(wo_sb[:], wo.rearrange("(h p) d -> p h d", p=2 * DH)).then_inc(loaded["late"], 16)
            sp.dma_start(we_sb[:], expert_w).then_inc(loaded["late"], 16)
            sp.dma_start(gate_sb[:], gate).then_inc(loaded["late"], 16)
            sp.dma_start(eb_sb[:], expert_b).then_inc(loaded["late"], 16)

            def feed(j, hp, b, s):
                if not (isinstance(s, int) and s < 2):
                    sp.wait_ge(q_turned, s - 1)
                sp.dma_start(q_feed[b][:].bitcast(f32).rearrange("p h d -> p (h d)"),
                             q_split[:, j % 2, b].bitcast(f32).rearrange("p n h s d -> p (n h s d)")
                             [:, bass.ds(hp * 4 * DH, 4 * DH)]).then_inc(q_fed[b], 16)

            def store(t):
                for b in range(B):
                    if t == TILES - 1:
                        sp.wait_ge(out_last, b + 1)
                    else:
                        sp.wait_ge(out_ready, B * t + b + 1)
                    sp.dma_start(out[b, t * T:(t + 1) * T, :], (y_last if t == TILES - 1 else out_sb)[b][:]).then_inc(stored, 16)

            for j in range(TILES):
                if j >= 1:
                    sp.wait_ge(q_ready, (j - 1) * STEPS + 2)
                for b in range(B):
                    if j == 0:
                        sp.wait_ge(wide_ready, b + 1)
                    feed(j, 0, b, j * STEPS + b)
                if j >= 1:
                    sp.wait_ge(q_ready, (j - 1) * STEPS + PAIRS)
                with sp.Fori(1, PAIRS // 2) as hp:
                    for b in range(B):
                        feed(j, hp, b, hp * 2 + (j * STEPS + b))
                if j == 0:
                    sp.wait_ge(wide_ready, 4)
                else:
                    sp.wait_ge(q_ready, j * STEPS)
                with sp.Fori(PAIRS // 2, PAIRS) as hp:
                    for b in range(B):
                        feed(j, hp, b, hp * 2 + (j * STEPS + b))
                if j >= 3:
                    store(j - 3)
            for t in range(TILES - 3, TILES):
                store(t)
            sp.wait_ge(stored, 16 * B * TILES)

        @block.tensor
        def _(pe):
            def fill(free, count):
                if not (isinstance(count, int) and count < 1):
                    pe.wait_ge(free, count)

            def queries(s, b):
                exact = isinstance(s, int)
                if not (exact and s < 1):
                    if exact and s > TOTAL:
                        pe.wait_ge(cols_ready, s - 3)
                    else:
                        pe.wait_ge(qT_ready, s)
                turned = q_ps[:].bitcast(f32r)
                if not (exact and s >= TOTAL):
                    pe.wait_ge(q_fed[b], s * 8 + (16 - 8 * b))
                    nc.tensor.transpose(turned[:, 0:T], q_feed[b][:, 0, :], ident_r[:])
                    last = nc.tensor.transpose(turned[:, T:2 * T], q_feed[b][:, 1, :], ident_r[:])
                if not (exact and s < 3):
                    pe.wait_ge(rows_ready, s - 2)
                    last = nc.tensor.transpose(q_ps[:, 2 * T:3 * T],
                                               recip_rows[1 - b][:].rearrange("p h d -> p (h d)"), ident_sb[:])
                last.then_inc(q_turned, 1)

            def qk(j, s, b, h):
                if h == 0:
                    pe.wait_ge(qT_ready, s + 1)
                if not (isinstance(s, int) and s < 1):
                    pe.wait_ge(probs[h], s)
                width = blocks(j) * T
                at, pieces = score_chunks(j)
                for c0, c1 in pieces:
                    nc.tensor.matmul(S[h][:, at + c0:at + c1], qT[b][:, h, :], k_stack[:, 0, b, c0:c1],
                                     start=True, stop=False)
                    nc.tensor.matmul(S[h][:, at + c0:at + c1], qT[b][:, h, :], k_stack[:, 1, b, c0:c1],
                                     start=False, stop=(c1 < width))
                nc.tensor.matmul(S[h][:, at + width - T:at + width], ident_bf[:], mask_bf[:],
                                 start=False, stop=True).then_inc(scores[h], 1)

            def turn_probs(j, s, step, h):
                a, b = bank_counts(j, step)
                pe.wait_ge(probs[h], s + 1)
                nb = blocks(j)
                if uses(j) == 1:
                    chunks = [((bankA, bankB)[h], (fullA, fullB)[h], (freeA, freeB)[h], (a, b)[h], 0, nb)]
                else:
                    chunks = [(bankA, fullA, freeA, a + h, 0, first_part(j)),
                              (bankB, fullB, freeB, b + h, first_part(j), nb)]
                for bank_, full, free, count, k0, k1 in chunks:
                    fill(free, count)
                    for k in range(k0, k1):
                        last = nc.tensor.transpose(bank_[:, (k - k0) * T:(k - k0 + 1) * T],
                                                   P[h][:, k * T:(k + 1) * T], ident_sb[:])
                    last.then_inc(full, 1)

            def product_read(j, step):
                if isinstance(step, int) and step == 0:
                    if j >= 3:
                        pe.wait_ge(y_added, added(j - 3, STEPS))
                elif j >= 2:
                    pe.wait_ge(y_added, step + added(j - 2, 0))

            def side_work(j, s, step, hp, b, last_in_bank):
                if not (isinstance(s, int) and s < 1):
                    if isinstance(s, int) and s == 1:
                        pe.wait_ge(rope_parts, 1)
                    else:
                        pe.wait_ge(o_free, s - 1)
                product_read(j, step)
                if j + 1 < TILES:
                    ins = nc.tensor.matmul(o_query, h1T[:, (j + 1) % 2, b, :], wq_sb[:, bass.ds(hp * 2 * DH, 2 * DH)],
                                           start=True, stop=True)
                    if last_in_bank:
                        ins.then_inc(o_full, 1)
                if j >= 2:
                    nc.tensor.matmul(o_expert, h2T[:, j % 2, b, :], we_sb[:, bass.ds(hp * DIM, DIM)],
                                     start=True, stop=True)

            def pv(j, step, b):
                a_count, b_count = bank_counts(j, step)
                pe.wait_ge(freeA, a_count + uses(j))
                pe.wait_ge(freeB, b_count + uses(j))
                nb = blocks(j)
                for k in range(nb):
                    for h in range(2):
                        last = nc.tensor.matmul(o_out[h * DH:(h + 1) * DH, :], v_sb[:, b, k, :],
                                                PT[b][h][:, k * T:(k + 1) * T],
                                                start=(k == 0), stop=(k == nb - 1))
                last.then_inc(o_full, 1)

            def stage(name, t):
                a, b = AT_STAGE[name, t]
                if name == "norm1_T":
                    pe.wait_ge(normed1_ready, t + 1)
                    fill(freeB, b)
                    for i in range(B):
                        last = nc.tensor.transpose(bankB[:, i * T:(i + 1) * T], normed1[:, i, :], ident_sb[:])
                    last.then_inc(fullB, 1)
                elif name == "kv":
                    pe.wait_ge(freeB, AT_STAGE["norm1_T", t][1] + 1)
                    fill(freeB, b)
                    for i in range(B):
                        last = nc.tensor.matmul(bankB[:, i * 2 * DH:(i + 1) * 2 * DH], h1T[:, t % 2, i, :], wkv_sb[:],
                                                start=True, stop=True)
                    last.then_inc(fullB, 1)
                elif name in ("q_first", "q_second"):
                    c = int(name == "q_second")
                    for i, (bank_, full, free, count) in enumerate(((bankA, fullA, freeA, a), (bankB, fullB, freeB, b))):
                        fill(free, count)
                        nc.tensor.matmul(bank_[:], h1T[:, 0, i, :], wq_sb[:, c * BANK:(c + 1) * BANK],
                                         start=True, stop=True).then_inc(full, 1)
                elif name == "k_T":
                    pe.wait_ge(k_ready, t + 1)
                    fill(freeA, a)
                    for k in range(2):
                        for i in range(B):
                            last = nc.tensor.transpose(
                                bankA[:, (2 * k + i) * T:(2 * k + i + 1) * T].bitcast(f32r),
                                k_split[:, i, k:k + 2, :].rearrange("p s d -> p (s d)"), ident_r[:])
                    last.then_inc(fullA, 1)
                elif name == "wo":
                    pe.wait_ge(o_free, (t + 1) * STEPS)
                    fill(freeA, a)
                    for i in range(B):
                        for hp in range(PAIRS):
                            last = nc.tensor.matmul(bankA[:, i * DIM:(i + 1) * DIM], oT[t % 2][:, i, hp, :],
                                                    wo_sb[:, hp, :], start=(hp == 0), stop=(hp == PAIRS - 1))
                    last.then_inc(fullA, 1)
                elif name == "norm2_T":
                    pe.wait_ge(normed2_ready, t + 1)
                    fill(freeB, b)
                    for i in range(B):
                        last = nc.tensor.transpose(bankB[:, i * T:(i + 1) * T], normed2[:, i, :], ident_sb[:])
                    last.then_inc(fullB, 1)
                elif name == "router":
                    nb_ = AT_STAGE["norm2_T", t][1]
                    pe.wait_ge(freeB, nb_ + 1)
                    fill(freeA, a)
                    for i in range(B):
                        last = nc.tensor.matmul(bankA[:, i * EXPERTS:(i + 1) * EXPERTS], h2T[:, t % 2, i, :], gate_sb[:],
                                                start=True, stop=True)
                    last.then_inc(fullA, 1)
                elif name == "comb_T":
                    pe.wait_ge(comb_ready, t + 1)
                    fill(freeB, b)
                    for i in range(B):
                        last = nc.tensor.transpose(bankB[0:EXPERTS, i * T:(i + 1) * T], comb[t % 2][:, i, :], ident_sb[:])
                    last.then_inc(fullB, 1)
                elif name == "bias":
                    pe.wait_ge(freeB, AT_STAGE["comb_T", t][1] + 1)
                    fill(freeA, a)
                    for i in range(B):
                        last = nc.tensor.matmul(bankA[:, i * DIM:(i + 1) * DIM], combT[:, i, :], eb_sb[:],
                                                start=True, stop=True)
                    last.then_inc(fullA, 1)

            def last_products(t, half, b):
                if t == TILES - 2 and half == 1 and b == 1:
                    pe.wait_ge(cols_ready, TOTAL)
                if t == TILES - 1 and half == 1:
                    pe.wait_ge(summed, summed_before(t - 1, 4 * b + 3, 0) + 1)
                nc.tensor.matmul(last_bank(t, half, b), h2T[:, t % 2, b, :], we_sb[:, half * BANK:(half + 1) * BANK],
                                 start=True, stop=True).then_inc(products, 1)

            def last_projection(b, first, end):
                pe.wait_ge(o_free, TOTAL - 2)
                for hp in range(first, end):
                    last = nc.tensor.matmul(S[b][:, 0:DIM], oT[(TILES - 1) % 2][:, b, hp, :], wo_sb[:, hp, :],
                                            start=(hp == 0), stop=(hp == PAIRS - 1))
                if end == PAIRS:
                    last.then_inc(wo_last, 1)

            def one_step(j, step, at, hp, b, prev, nxt):
                s = step + j * STEPS
                queries(s + 2, b)
                for h in range(2):
                    if nxt is not None:
                        qk(nxt, s + 1, 1 - b, h)
                    turn_probs(j, s, at, h)
                    if h == 0 and isinstance(s, int) and s == TOTAL - 1:
                        last_projection(0, 0, PAIRS - 1)
                side_work(j, s, step, hp, b, prev is None)
                if prev is not None:
                    pv(prev[0], prev[1], 1 - b)

            pe.wait_ge(silu_ready, 1)
            pe.wait_ge(loaded["mod"], 16)
            for n, m in enumerate((SA, CA, SB, CB)):
                last = nc.tensor.matmul(bankA[:, n * B:(n + 1) * B], wmod_sb[:, m * DIM:(m + 1) * DIM],
                                        silu[:, 2, :], start=True, stop=True)
            last.then_inc(fullA, 1)
            pe.wait_ge(loaded["consts"], 16)
            for name, t in HEAD[:-1]:
                if name in ("kv", "q_first"):
                    pe.wait_ge(loaded["wkv" if name == "kv" else "wq"], 16)
                stage(name, t)
                if name == "q_first":
                    for n, m in enumerate((GA, GB)):
                        for i in range(B):
                            last = nc.tensor.matmul(S[1][:, (n * B + i) * DIM:(n * B + i + 1) * DIM],
                                                    silu_rows[:, i, :], wmod_sb[:, m * DIM:(m + 1) * DIM],
                                                    start=True, stop=True)
                    last.then_inc(gates_full, 1)
            queries(0, 0)
            queries(1, 1)
            ka, kb = AT_STAGE["k_T", 0]
            pe.wait_ge(freeA, ka + 1)
            pe.wait_ge(masks_ready, 1)
            qk(0, 0, 0, 0)
            pe.wait_ge(gates_read, 1)
            qk(0, 0, 0, 1)
            stage(*HEAD[-1])
            for j in range(TILES):
                for step in plan(j):
                    if isinstance(step, tuple):
                        with pe.Fori(step[0] // 2, step[1] // 2) as hp:
                            for b in range(B):
                                at = hp * 2 + b
                                one_step(j, at, (at, step[0]), hp, b, (j, (at - 1, step[0])), j)
                        continue
                    prev = (j, step - 1) if step else ((j - 1, STEPS - 1) if j else None)
                    nxt = j if step < STEPS - 1 else (j + 1 if j + 1 < TILES else None)
                    if step == STEPS - 1 and nxt is not None:
                        pe.wait_ge(freeA, AT_STAGE["k_T", nxt][0] + 1)
                    one_step(j, step, step, step // 2, step % 2, prev, nxt)
                    if step == 0 and j == 1:
                        pe.wait_ge(loaded["late"], 64)
                    for name, t in stages(j, step):
                        stage(name, t)
            last_projection(1, 0, 3)
            pe.wait_ge(o_free, TOTAL - 1)
            last_projection(0, PAIRS - 1, PAIRS)
            pe.wait_ge(y_added, added(TILES - 3, STEPS))
            queries(TOTAL + 2, 0)
            pv(TILES - 1, STEPS - 1, 1)
            stage("comb_T", TILES - 2)
            last_projection(1, 3, PAIRS - 1)
            pe.wait_ge(o_free, TOTAL)
            last_projection(1, PAIRS - 1, PAIRS)
            stage("bias", TILES - 2)
            for b in range(B):
                last_products(TILES - 2, 0, b)
            last_products(TILES - 2, 1, 0)
            stage("norm2_T", TILES - 1)
            last_products(TILES - 2, 1, 1)
            stage("router", TILES - 1)
            pe.wait_ge(attn_last, B)
            for b in range(B):
                last_products(TILES - 1, 0, b)
            last_products(TILES - 1, 1, 0)
            stage("comb_T", TILES - 1)
            last_products(TILES - 1, 1, 1)
            pe.wait_ge(summed, summed_before(TILES - 2, 3, 1) + 1)
            pe.wait_ge(freeB, AT_STAGE["comb_T", TILES - 1][1] + 1)
            for b, rest in enumerate((o_ps, q_ps)):
                if b == 1:
                    pe.wait_ge(summed, summed_before(TILES - 2, EXPERTS - 1, 1) + 1)
                nc.tensor.matmul(rest[:, 0:DIM], combT[:, b, :], eb_sb[:], start=True, stop=False)
                for e in range(4):
                    pe.wait_ge(scaled_ready, b * 4 + e + 1)
                    last = nc.tensor.matmul(rest[:, 0:DIM], ident_sb[:], scaled[:, b, e, :],
                                            start=False, stop=(e == 3))
                last.then_inc(rest_summed, 1)

        @block.scalar
        def _(act):
            act.dma_start(c_sb[:], c_t).then_inc(loaded["c"], 16)

            def turn_queries(s, b):
                exact = isinstance(s, int)
                act.wait_ge(q_turned, s + 1)
                if not (exact and s < 3):
                    nc.scalar.copy(recip_cols[1 - b][:], q_ps[:, 2 * T:3 * T]).then_inc(cols_ready, 1)
                if not (exact and s >= TOTAL):
                    nc.scalar.copy(qT[b][:].rearrange("p h t -> p (h t)"), q_ps[:, 0:2 * T]).then_inc(qT_ready, 1)

            def keep_probs(j, s, at, b, h):
                a, bc = bank_counts(j, at)
                if uses(j) == 1 and h == 1:
                    if j < ACT_ALONE:
                        act.wait_ge(fullB, bc + 1)
                        if not (isinstance(s, int) and s < 2):
                            act.wait_ge(o_full, s)
                        nc.scalar.copy(PT[b][h][:, 0:blocks(j) * T], bankB[:, 0:blocks(j) * T]).then_inc(freeB, 1)
                    return
                cols = first_part(j) * T
                act.wait_ge(fullA, a + (h + 1))
                if not (isinstance(s, int) and s < 2):
                    act.wait_ge(o_full, s)
                nc.scalar.copy(PT[b][h][:, 0:cols], bankA[:, 0:cols]).then_inc(freeA, 1)

            def exponential(j, s, b, h, turned):
                act.wait_ge(least_ready[h], s + 1)
                if turned is not None:
                    act.wait_ge(*turned)
                width, at = blocks(j) * T, score_chunks(j)[0]
                nc.scalar.activation(P[h][:, 0:width], S[h][:, at:at + width], ACT.Exp,
                                     bias=least[:, h:h + 1], scale=-1.0,
                                     accum_out=sums[b][:, h:h + 1]).then_inc(probs[h], 1)

            def one_step(j, step, at, b, nxt):
                s = step + j * STEPS
                turn_queries(s + 2, b)
                a, bb = bank_counts(j, at)
                for h in range(2):
                    keep_probs(j, s, at, b, h)
                    if nxt is not None:
                        if uses(j) == 1:
                            turned = ((fullA, a + 1), (fullB, bb + 1))[h]
                        else:
                            turned = (fullB, bb + (h + 1))
                        if not (isinstance(s, int) and s < 1):
                            act.wait_ge(recips_ready, s)
                        exponential(nxt, s + 1, 1 - b, h, turned)

            def stage(name, t):
                a, b = AT_STAGE[name, t]
                if name == "norm1_T":
                    act.wait_ge(fullB, b + 1)
                    if t == 0:
                        act.wait_ge(freeA, 1)
                    for i in range(B):
                        last = nc.scalar.activation(h1T[:, t % 2, i, :], bankB[:, i * T:(i + 1) * T], ACT.Identity,
                                                    bias=mod_cols[:, 0, i:i + 1], scale=mod_cols[:, 1, i:i + 1])
                    last.then_inc(freeB, 1)
                elif name == "norm2_T":
                    act.wait_ge(fullB, b + 1)
                    for i in range(B):
                        last = nc.scalar.activation(h2T[:, t % 2, i, :], bankB[:, i * T:(i + 1) * T], ACT.Identity,
                                                    bias=mod_cols[:, 2, i:i + 1], scale=mod_cols[:, 3, i:i + 1])
                    last.then_inc(freeB, 1)
                elif name == "q_first":
                    wide_highs(0)
                elif name == "router":
                    act.wait_ge(sorted_ready, t + 1)
                    for i in range(B):
                        last = nc.scalar.activation(e_sorted[:, i, :], sorted_l[:, i, :], ACT.Exp,
                                                    bias=neg_top[:, i:i + 1], accum_out=e_sum[:, i:i + 1])
                    last.then_inc(router_exp, 1)
                elif name == "k_T":
                    act.wait_ge(fullA, a + 1)
                    nc.scalar.copy(k_stack[:, :, :, t * T:(t + 1) * T],
                                   bankA[:].rearrange("p (s b t) -> p s b t", s=2, b=B)).then_inc(freeA, 1)

            def wide_highs(c):
                for i in range(B):
                    act.wait_ge(wide_sum, 2 * c + i + 1)
                    nc.scalar.copy(q_split[:, 0, i, 4 * c:4 * c + 4, :, 0, :].rearrange("p n h d -> p (n h) d"),
                                   wide_cos[:, i]).then_inc(wide_high, 1)

            act.wait_ge(halves_ready, 1)
            nc.scalar.activation(unused[:], minus_half[:], ACT.Exp)
            act.wait_ge(loaded["c"], 16)
            nc.scalar.activation(silu[:, 0, :], c_sb[:], ACT.Exp, scale=-1.0).then_inc(silu_exp, 1)
            act.wait_ge(loaded["consts"], 16)
            nc.scalar.copy(ident_bf[:], ident_sb[:])
            nc.scalar.copy(ident_r[:], ident_sb[:])
            for name, t in HEAD[:-1]:
                stage(name, t)
                if name == "kv":
                    act.wait_ge(loaded["mask"], 16)
                    nc.scalar.copy(mask_bf[:], mask_sb[:]).then_inc(masks_ready, 1)
            turn_queries(0, 0)
            turn_queries(1, 1)
            for h in range(2):
                exponential(0, 0, 0, h, None)
            stage(*HEAD[-1])
            for j in range(TILES):
                for step in plan(j):
                    if isinstance(step, tuple):
                        with act.Fori(step[0] // 2, step[1] // 2) as hp:
                            for b in range(B):
                                one_step(j, hp * 2 + b, (hp * 2 + b, step[0]), b, j)
                        continue
                    nxt = j if step < STEPS - 1 else (j + 1 if j + 1 < TILES else None)
                    one_step(j, step, step, step % 2, nxt)
                    for name, t in stages(j, step):
                        stage(name, t)
                    if step == 1 and j == 0:
                        wide_highs(1)
            turn_queries(TOTAL + 2, 0)
            for name, t in TAIL:
                stage(name, t)
            act.wait_ge(comb_ready, TILES)
            for b in range(B):
                act.wait_ge(products, 4 + B + b + 1)
                for e in range(4):
                    nc.scalar.activation(scaled[:, b, e, :], last_bank(TILES - 1, 1, b)[:, e * DIM:(e + 1) * DIM],
                                         ACT.Copy, scale=comb[(TILES - 1) % 2][:, b, 4 + e:5 + e])\
                        .then_inc(scaled_ready, 1)

        @block.vector
        def _(dve):
            links = [0]

            def link(ins):
                links[0] += 1
                ins.then_inc(dve_link, 1)
                dve.wait_ge(dve_link, links[0])

            def smallest(j, s, h):
                dve.wait_ge(scores[h], s + 1)
                width, at = blocks(j) * T, score_chunks(j)[0]
                nc.vector.tensor_reduce(least[:, h:h + 1], S[h][:, at:at + width], AX.X, ALU.min)\
                    .then_inc(least_ready[h], 1)

            def keep_probs(j, s, at, b, h):
                _, bc = bank_counts(j, at)
                if (uses(j) == 1 and h == 0) or j < ACT_ALONE:
                    return
                first = 0 if uses(j) == 1 else first_part(j)
                cols = (blocks(j) - first) * T
                dve.wait_ge(fullB, bc + 1 if uses(j) == 1 else bc + (h + 1))
                if not (isinstance(s, int) and s < 2):
                    dve.wait_ge(o_full, s)
                nc.vector.tensor_copy(PT[b][h][:, first * T:first * T + cols], bankB[:, 0:cols]).then_inc(freeB, 1)

            def reciprocals(j, s, b):
                dve.wait_ge(probs[1], s + 1)
                if not (isinstance(s, int) and s < 2):
                    dve.wait_ge(rows_ready, s - 1)
                nc.vector.reciprocal(recips[b][:], sums[b][:]).then_inc(recips_ready, 1)
                if j < ROWS_BY_VECTOR:
                    dve.wait_ge(recips_ready, s + 1)
                    nc.vector.tensor_copy(recip_rows[b][:], recips[b][:].unsqueeze(2).to_broadcast([T, 2, DH]))\
                        .then_inc(rows_ready, 1)

            def expert(j, step, hp, b):
                dve.wait_ge(y_added, step + (added(j - 2, 0) - 1))
                nc.vector.scalar_tensor_tensor(out=y[b][:], in0=o_expert, scalar=comb[j % 2][:, b, bass.ds(hp, 1)],
                                               in1=y[b][:], op0=ALU.mult, op1=ALU.add).then_inc(y_added, 1)

            def later(j):
                return uses(j) == 2

            def one_step(j, step, at, hp, b, nxt, prev, prev_hp, before):
                s = step + j * STEPS
                for h in range(2):
                    if nxt is not None:
                        smallest(nxt, s + 1, h)
                    keep_probs(j, s, at, b, h)
                    if h == 0 and before is not None:
                        expert(*before)
                    if h == 0:
                        reciprocals(j, s, b)
                meanwhile(j, step)
                outputs(j, step, s, hp, b, prev, prev_hp)

            def outputs(j, step, s, hp, b, prev, prev_hp):
                dve.wait_ge(o_full, s + 1)
                if j + 1 < TILES:
                    if not (isinstance(s, int) and s < 2):
                        dve.wait_ge(q_ready, s - 1)
                    rope(o_query, rope_cos[:, b], rope_sin[:, b], cosq_sb[:, j + 1, :], sinq_sb[:, j + 1, :], 2)\
                        .then_inc(rope_parts, 1)
                if prev is not None:
                    dve.wait_ge(cols_ready, s)
                    nc.vector.tensor_tensor(oT[prev % 2][:, 1 - b].rearrange("p h t -> p (h t)")
                                            [:, bass.ds(prev_hp * T, T)],
                                            o_out, recip_cols[1 - b][:], ALU.mult).then_inc(o_free, 1)
                if 2 <= j < TILES and not later(j) and not (isinstance(step, int) and step == 0):
                    expert(j, step, hp, b)

            def norm_stats(tiles, stats_, mean_var_):
                for i in range(B):
                    last = nc.vector.bn_stats(stats_[:, i, :], tiles[:, i, :])
                link(last)
                for i in range(B):
                    last = nc.vector.bn_aggr(mean_var_[:, i, :], stats_[:, i, :])
                last.then_inc(stats_ready, 1)

            def normalise(tiles, dst, mean_var_, rstd_, ready):
                for i in range(B):
                    last = nc.vector.tensor_scalar(dst[:, i, :], tiles[:, i, :], mean_var_[:, i, 0:1],
                                                   rstd_[:, i:i + 1], ALU.subtract, ALU.mult)
                last.then_inc(ready, 1)

            def norm1_stats(t):
                if t < TILES:
                    norm_stats(x_sb[:, :, t, :], stats, mean_var)

            def norm1(t):
                if t < TILES:
                    dve.wait_ge(rstd_ready, RSTD[1, t])
                    if t >= 1:
                        dve.wait_ge(fullB, AT_STAGE["norm1_T", t - 1][1] + 1)
                    normalise(x_sb[:, :, t, :], normed1, mean_var, rstd, normed1_ready)

            def norm2_stats(t):
                dve.wait_ge(x1_ready, t + 1)
                norm_stats(x_sb[:, :, t, :], stats2, mean_var2)

            def norm2(t):
                dve.wait_ge(rstd_ready, RSTD[2, t])
                normalise(x_sb[:, :, t, :], normed2, mean_var2, rstd2, normed2_ready)

            def rope(columns, dst_cos, dst_sin, cos, sin, heads):
                nc.vector.tensor_tensor(dst_cos, columns.rearrange("p (h d) -> p h d", d=DH),
                                        cos.unsqueeze(1).to_broadcast([T, heads, DH]), ALU.mult)
                return nc.vector.tensor_tensor(
                    dst_sin.rearrange("p h (x d) -> p h x d", x=2), halves_swapped(columns),
                    sin.rearrange("p (x d) -> p x d", x=2).unsqueeze(1).to_broadcast([T, heads, 2, HALF]), ALU.mult)

            def wide_low(c, i):
                dve.wait_ge(wide_high, 2 * c + i + 1)
                heads = q_split[:, 0, i, 4 * c:4 * c + 4]
                nc.vector.tensor_tensor(heads[:, :, :, 1, :].rearrange("p n h d -> p (n h) d"), wide_cos[:, i],
                                        heads[:, :, :, 0, :].rearrange("p n h d -> p (n h) d").bitcast(f32),
                                        ALU.subtract).then_inc(wide_ready, 1)

            def stage(name, t):
                a, b = AT_STAGE[name, t]
                if name == "kv":
                    dve.wait_ge(fullB, b + 1)
                    kv = bankB[:, 0:B * 2 * DH].rearrange("p (b d) -> p b d", b=B)
                    nc.vector.tensor_copy(v_sb[:, :, t, :], kv[:, :, DH:2 * DH])
                    if t >= 1:
                        dve.wait_ge(k_ready, t)
                    for i in range(B):
                        last = rope(bankB[:, i * 2 * DH:i * 2 * DH + DH], k_cos[:, i:i + 1], k_sin[:, i:i + 1],
                                    cosk_sb[:, t, :], sink_sb[:, t, :], 1)
                    last.then_inc(freeB, 1)
                elif name in ("q_first", "q_second"):
                    c = int(name == "q_second")
                    for i, (bank_, full, free, count) in enumerate(((bankA, fullA, freeA, a), (bankB, fullB, freeB, b))):
                        dve.wait_ge(full, count + 1)
                        if c == 1:
                            dve.wait_ge(wide_ready, i + 1)
                        rope(bank_[:], wide_cos[:, i], wide_sin[:, i], cosq_sb[:, 0, :], sinq_sb[:, 0, :], 8)\
                            .then_inc(free, 1)
                    if c == 0:
                        for i in range(B):
                            wide_low(0, i)
                elif name == "wo":
                    dve.wait_ge(fullA, a + 1)
                    nc.vector.tensor_tensor(attn[:], bankA[:, 0:B * DIM].rearrange("p (b d) -> p b d", b=B),
                                            gates[:, 0], ALU.mult).then_inc(freeA, 1)
                elif name == "router":
                    dve.wait_ge(fullA, a + 1)
                    nc.vector.tensor_copy(logits[:], bankA[:, 0:B * EXPERTS].rearrange("p (b e) -> p b e", b=B))\
                        .then_inc(freeA, 1)
                    dve.wait_ge(freeA, a + 1)
                    for i in range(B):
                        last = nc.vector.max(sorted_l[:, i, :], logits[:, i, :])
                    link(last)
                    nc.vector.tensor_scalar(neg_top[:], sorted_l[:, :, 0], -1.0, None, ALU.mult).then_inc(sorted_ready, 1)
                    for i in range(B):
                        last = nc.vector.max_index(top_idx[:, i, :], sorted_l[:, i, :], logits[:, i, :])
                    link(last)
                    link(nc.vector.tensor_copy(top_idx_f[:], top_idx[:]))
                elif name == "comb_T":
                    dve.wait_ge(fullB, b + 1)
                    nc.vector.tensor_copy(combT[:], bankB[0:EXPERTS, 0:B * T].rearrange("p (b t) -> p b t", b=B))\
                        .then_inc(freeB, 1)
                elif name == "bias":
                    dve.wait_ge(fullA, a + 1)
                    if t < TILES - 2:
                        open_ = 1 if later(t + 2) and t + 2 < TILES - 1 else 0
                        dve.wait_ge(y_added, added(t, STEPS - open_))
                        for i in range(B):
                            last = nc.vector.tensor_tensor(y[i][:], y[i][:], bankA[:, i * DIM:(i + 1) * DIM], ALU.add)
                    else:
                        for i in range(B):
                            last = nc.vector.tensor_copy(y[i][:], bankA[:, i * DIM:(i + 1) * DIM])
                    last.then_inc(freeA, 1)
                    dve.wait_ge(freeA, a + 1)

            def sum_products(t, first, end):
                for e in range(first, end):
                    for i in range(B):
                        n = summed_before(t, e, i)
                        if e % 4 == 0:
                            dve.wait_ge(products, (t - (TILES - 2)) * 4 + e // 4 * B + i + 1)
                        to = (y if t == TILES - 2 else y_last)[i]
                        column = last_bank(t, e // 4, i)[:, e % 4 * DIM:(e % 4 + 1) * DIM]
                        weight = comb[t % 2][:, i, e:e + 1]
                        if t == TILES - 1 and e == 0:
                            ins = nc.vector.tensor_scalar(to[:], column, weight, None, ALU.mult)
                        else:
                            if n >= B:
                                dve.wait_ge(summed, n - 1)
                            ins = nc.vector.scalar_tensor_tensor(out=to[:], in0=column, scalar=weight, in1=to[:],
                                                                 op0=ALU.mult, op1=ALU.add)
                        ins.then_inc(summed, 1)

            def gate_y(t, i):
                if t >= 1:
                    dve.wait_ge(out_ready, B * (t - 1) + i + 1)
                nc.vector.tensor_tensor(y_gated[i][:], y[i][:], gates[:, 1, i, :], ALU.mult).then_inc(y_ready, 1)

            def top_weights(t):
                dve.wait_ge(router_exp, t + 1)
                link(nc.vector.reciprocal(e_rec[:], e_sum[:]))
                link(nc.vector.tensor_tensor(top_w[:], e_sorted[:, :, 0:TOPK],
                                             e_rec[:].unsqueeze(2).to_broadcast([T, B, TOPK]), ALU.mult))
                every = [T, B, TOPK, EXPERTS]
                link(nc.vector.tensor_tensor(comb_k[:], iota_sb[:].unsqueeze(1).unsqueeze(1).to_broadcast(every),
                                             top_idx_f[:, :, 0:TOPK].unsqueeze(3).to_broadcast(every), ALU.is_equal))
                link(nc.vector.tensor_tensor(comb_k[:], comb_k[:], top_w[:].unsqueeze(3).to_broadcast(every), ALU.mult))

            def combine_weights(t):
                if t >= 2:
                    dve.wait_ge(y_ready, B * (t - 1))
                    dve.wait_ge(fullB, AT_STAGE["comb_T", t - 2][1] + 1)
                nc.vector.tensor_tensor(comb[t % 2][:], comb_k[:, :, 0, :], comb_k[:, :, 1, :], ALU.add).then_inc(comb_ready, 1)
                dve.wait_ge(comb_ready, t + 1)

            dve.wait_ge(loaded["x0"], 16 * B)
            norm1_stats(0)
            dve.wait_ge(silu_exp, 1)
            link(nc.vector.tensor_scalar_add(silu[:, 1, :], silu[:, 0, :], 1.0))
            link(nc.vector.reciprocal(silu[:, 0, :], silu[:, 1, :]))
            link(nc.vector.tensor_tensor(silu[:, 2, :], silu[:, 0, :], c_sb[:], ALU.mult))
            nc.vector.tensor_copy(silu_rows[:], silu[:, 2, :].unsqueeze(2).to_broadcast([DIM, B, T])).then_inc(silu_ready, 1)
            norm1(0)
            dve.wait_ge(fullA, 1)
            cols = bankA[:, 0:4 * B].rearrange("p (m b) -> p m b", b=B)
            nc.vector.tensor_copy(mod_cols[:, 0:4:2, :], cols[:, 0:4:2, :])
            nc.vector.tensor_scalar_add(mod_cols[:, 1:4:2, :], cols[:, 1:4:2, :], 1.0).then_inc(freeA, 1)
            norm1_stats(1)
            dve.wait_ge(loaded["tables0"], 64)
            for name, t in HEAD:
                if (name, t) == ("norm1_T", 1):
                    dve.wait_ge(loaded["tables"], 64)
                    norm1(1)
                    dve.wait_ge(gates_full, 1)
                    nc.vector.tensor_copy(gate_tmp[:, 2, :], S[1][:, 0:BANK]).then_inc(gates_read, 1)
                stage(name, t)
            for h in range(2):
                smallest(0, 0, h)

            def meanwhile(j, step):
                if not isinstance(step, int):
                    return
                if step == 0 and j >= 3:
                    dve.wait_ge(y_added, added(j - 3, STEPS))
                    for i in range(B):
                        gate_y(j - 3, i)
                if step == 0 and j >= 2:
                    combine_weights(j - 2)
                    for i in range(B):
                        nc.vector.memset(y[i][:], 0.0).then_inc(y_added, 1)
                if step == 8 and j >= 1:
                    norm2_stats(j - 1)
                if step == 9 and j >= 1:
                    norm2(j - 1)
                if step == 9:
                    norm1_stats(j + 2)
                if step == 14:
                    norm1(j + 2)
                if step in (8, 14, 15) and j == 0:
                    gate_rows((8, 14, 15).index(step))
                if step == STEPS - 1 and 1 <= j < TILES - 1:
                    top_weights(j - 1)

            def gate_rows(part):
                g = gate_tmp[:, 2, :]
                if part == 0:
                    link(nc.vector.tensor_scalar(gate_tmp[:, 0, :], g, -1.0, None, ALU.mult))
                    link(nc.vector.tensor_tensor(gate_tmp[:, 1, :], g, gate_tmp[:, 0, :], ALU.max))
                elif part == 1:
                    link(nc.vector.tensor_scalar(gate_tmp[:, 1, :], gate_tmp[:, 1, :], 0.25, None, ALU.max))
                    link(nc.vector.tensor_scalar(gate_tmp[:, 0, :], g, 0.0, 2.0, ALU.is_ge, ALU.mult))
                else:
                    link(nc.vector.tensor_scalar(gate_tmp[:, 0, :], gate_tmp[:, 0, :], -1.0, None, ALU.add))
                    link(nc.vector.tensor_tensor(gates[:].rearrange("p g b d -> p (g b d)"), gate_tmp[:, 0, :],
                                                 gate_tmp[:, 1, :], ALU.mult))

            for j in range(TILES):
                for step in plan(j):
                    if isinstance(step, tuple):
                        with dve.Fori(step[0] // 2, step[1] // 2) as hp:
                            for b in range(B):
                                one_step(j, hp * 2 + b, (hp * 2 + b, step[0]), hp, b, j, j, hp - (1 - b),
                                         (j, hp * 2 + (b - 1), hp - (1 - b), 1 - b) if later(j) else None)
                        continue
                    prev = j if step else (j - 1 if j else None)
                    prev_hp = (step - 1) // 2 if step else PAIRS - 1
                    nxt = j if step < STEPS - 1 else (j + 1 if j + 1 < TILES else None)
                    before = None
                    if step and later(j):
                        before = (j, step - 1, (step - 1) // 2, 1 - step % 2)
                    elif not step and j and later(j - 1):
                        before = (j - 1, STEPS - 1, PAIRS - 1, 1)
                    one_step(j, step, step, step // 2, step % 2, nxt, prev, prev_hp, before)
                    if step == 0 and j == 0:
                        dve.wait_ge(loaded["x1"], 16 * B)
                        dve.wait_ge(consts_ready, 1)
                    if j * STEPS + step == TOTAL - 1:
                        expert(j, step, PAIRS - 1, 1)
                    for name, t in stages(j, step):
                        stage(name, t)
                    if step == 0 and j >= 2 and not later(j):
                        expert(j, 0, 0, 0)
                    if step == 1 and j == 0:
                        for i in range(B):
                            wide_low(1, i)
            dve.wait_ge(y_added, added(TILES - 3, STEPS))
            for i in range(B):
                gate_y(TILES - 3, i)

            def last_attention(i):
                tile_ = x_sb[:, i, TILES - 1, :]
                dve.wait_ge(wo_last, i + 1)
                nc.vector.tensor_tensor(attn[:, i, :], S[i][:, 0:DIM], gates[:, 0, i, :], ALU.mult)\
                    .then_inc(attn_last, 1)
                dve.wait_ge(attn_last, i + 1)
                nc.vector.tensor_tensor(tile_, tile_, attn[:, i, :], ALU.add).then_inc(x1_last, 1)
                dve.wait_ge(x1_last, i + 1)
                link(nc.vector.bn_stats(stats2[:, i, :], tile_))
                ins = nc.vector.bn_aggr(mean_var2[:, i, :], stats2[:, i, :])
                if i == B - 1:
                    ins.then_inc(stats_ready, 1)

            dve.wait_ge(x1_ready, TILES - 1)
            last_attention(0)
            top_weights(TILES - 2)
            combine_weights(TILES - 2)
            outputs(TILES - 1, STEPS, TOTAL, None, 0, TILES - 1, PAIRS - 1)
            stage("comb_T", TILES - 2)
            last_attention(1)
            stage("bias", TILES - 2)
            norm2(TILES - 1)
            sum_products(TILES - 2, 0, 4)
            stage("router", TILES - 1)
            sum_products(TILES - 2, 4, 6)
            top_weights(TILES - 1)
            combine_weights(TILES - 1)
            sum_products(TILES - 2, 6, EXPERTS)
            stage("comb_T", TILES - 1)
            dve.wait_ge(summed, summed_before(TILES - 1, 0, 0))
            for i in range(B):
                gate_y(TILES - 2, i)
            sum_products(TILES - 1, 0, 4)
            dve.wait_ge(summed, summed_before(TILES - 1, 4, 0))
            for i in range(B):
                dve.wait_ge(rest_summed, i + 1)
                nc.vector.tensor_tensor(y_last[i][:], y_last[i][:], (o_ps, q_ps)[i][:, 0:DIM], ALU.add)\
                    .then_inc(finishing, 1)
            for i in range(B):
                dve.wait_ge(finishing, i + 1)
                nc.vector.tensor_tensor(y_last[i][:], y_last[i][:], gates[:, 1, i, :], ALU.mult).then_inc(finishing, 1)
            for i in range(B):
                dve.wait_ge(finishing, B + i + 1)
                nc.vector.tensor_tensor(y_last[i][:], y_last[i][:], x_sb[:, i, TILES - 1, :], ALU.add)\
                    .then_inc(out_last, 1)

        @block.gpsimd
        def _(pool):
            links = [0]

            def link(ins):
                links[0] += 1
                ins.then_inc(pool_link, 1)
                pool.wait_ge(pool_link, links[0])

            def inverse_deviation(count, mean_var_, var_eps_, rstd_):
                pool.wait_ge(stats_ready, count)
                link(nc.gpsimd.tensor_scalar(var_eps_[:], mean_var_[:, :, 1], EPS, None, ALU.add))
                nc.gpsimd.tensor_tensor(rstd_[:], var_eps_[:], minus_half[:], ALU.pow).then_inc(rstd_ready, 1)

            def keys(t):
                pool.wait_ge(freeB, AT_STAGE["kv", t][1] + 1)
                if t >= 1:
                    pool.wait_ge(fullA, AT_STAGE["k_T", t - 1][0] + 1)
                link(nc.gpsimd.tensor_tensor(k_cos[:], k_cos[:], k_sin[:], ALU.add))
                nc.gpsimd.tensor_copy(k_split[:, :, 2, :], k_cos[:])
                link(nc.gpsimd.tensor_copy(k_split[:, :, 0, :], k_cos[:]))
                nc.gpsimd.tensor_tensor(k_split[:, :, 1, :], k_cos[:], k_split[:, :, 0, :].bitcast(f32),
                                        ALU.subtract).then_inc(k_ready, 1)

            def wide_queries(c):
                for i in range(B):
                    a, b = AT_STAGE[("q_first", "q_second")[c], 0]
                    pool.wait_ge((freeA, freeB)[i], (a, b)[i] + 1)
                    nc.gpsimd.tensor_tensor(wide_cos[:, i], wide_cos[:, i], wide_sin[:, i], ALU.add).then_inc(wide_sum, 1)

            def query_pair(j, step, hp, b):
                n = step + (j * STEPS + 1)
                pool.wait_ge(rope_parts, n)
                nc.gpsimd.tensor_tensor(rope_cos[:, b], rope_cos[:, b], rope_sin[:, b], ALU.add).then_inc(rope_sum, 1)
                pair = q_split[:, (j + 1) % 2, b, bass.ds(hp, 1)]
                pool.wait_ge(rope_sum, n)
                nc.gpsimd.tensor_copy(pair[:, :, :, 0, :], rope_cos[:, b].unsqueeze(1)).then_inc(rope_high, 1)
                pool.wait_ge(rope_high, n)
                nc.gpsimd.tensor_tensor(pair[:, :, :, 1, :], rope_cos[:, b].unsqueeze(1),
                                        pair[:, :, :, 0, :].bitcast(f32), ALU.subtract).then_inc(q_ready, 1)

            def rows(s, b):
                pool.wait_ge(recips_ready, s + 1)
                if not (isinstance(s, int) and s < 2):
                    pool.wait_ge(o_full, s)
                nc.gpsimd.tensor_tensor(recip_rows[b][:], recips[b][:].unsqueeze(2).to_broadcast([T, 2, DH]),
                                        ones[:], ALU.mult).then_inc(rows_ready, 1)

            def residual(t):
                pool.wait_ge(freeA, AT_STAGE["wo", t][0] + 1)
                nc.gpsimd.tensor_tensor(x_sb[:, :, t, :], x_sb[:, :, t, :], attn[:], ALU.add).then_inc(x1_ready, 1)

            def result(t, i):
                pool.wait_ge(y_ready, B * t + i + 1)
                if t >= 1:
                    pool.wait_ge(stored, 16 * B * t)
                nc.gpsimd.tensor_tensor(out_sb[i][:], y_gated[i][:], x_sb[:, i, t, :], ALU.add).then_inc(out_ready, 1)

            nc.gpsimd.memset(minus_half[:], -0.5).then_inc(halves_ready, 1)
            pool.wait_ge(halves_ready, 1)
            link(nc.gpsimd.memset(ones[:], 1.0))
            nc.gpsimd.iota(iota_sb[:], pattern=[[1, EXPERTS]], base=0, channel_multiplier=0,
                           allow_small_or_imprecise_dtypes=True).then_inc(consts_ready, 1)
            inverse_deviation(RSTD[1, 0], mean_var, var_eps, rstd)
            inverse_deviation(RSTD[1, 1], mean_var, var_eps, rstd)
            keys(0)
            wide_queries(0)
            for j in range(TILES):
                if 1 <= j < TILES - 1:
                    pool.wait_ge(q_turned, j * STEPS)
                for step in plan(j):
                    if isinstance(step, tuple):
                        with pool.Fori(step[0] // 2, step[1] // 2) as hp:
                            for b in range(B):
                                if j >= ROWS_BY_VECTOR:
                                    rows(hp * 2 + (j * STEPS + b), b)
                                if j + 1 < TILES:
                                    query_pair(j, hp * 2 + b, hp, b)
                        continue
                    if j >= ROWS_BY_VECTOR:
                        rows(j * STEPS + step, step % 2)
                    if step == 8 and j >= 1:
                        inverse_deviation(RSTD[2, j - 1], mean_var2, var_eps2, rstd2)
                    if step == 9 and j + 2 < TILES:
                        inverse_deviation(RSTD[1, j + 2], mean_var, var_eps, rstd)
                    if j + 1 < TILES:
                        query_pair(j, step, step // 2, step % 2)
                    if step == 0 and j == 0:
                        wide_queries(1)
                    if step == 0 and j + 1 < TILES:
                        keys(j + 1)
                    if step == 9 and j >= 3:
                        for i in range(B):
                            result(j - 3, i)
                    if step == 1 and j >= 1:
                        residual(j - 1)
            for i in range(B):
                result(TILES - 3, i)
            inverse_deviation(RSTD[2, TILES - 1], mean_var2, var_eps2, rstd2)
            for i in range(B):
                result(TILES - 2, i)


def rope_tables():
    inv_freq = (1.0 / np.power(np.float32(10000.0), np.arange(0, DH, 2, dtype=np.float32) / np.float32(DH))).astype(np.float32)
    freqs = np.arange(N, dtype=np.float32)[:, None] * inv_freq[None, :]
    cos = np.cos(np.concatenate([freqs, freqs], axis=1)).astype(np.float32)
    sin = np.sin(np.concatenate([-freqs, freqs], axis=1)).astype(np.float32)
    s = np.float32(-SCALE)
    return cos * s, sin * s, cos, sin


def kernel(L0_attn_x, L0_attn_Wq, L0_attn_Wkv, L0_attn_Wo, L0_ffn_gate_w, L0_ffn_expert_w, L0_ffn_expert_b,
           L0_c, L0_wmod):
    import concourse.bacc as bacc
    from concourse.bass_utils import run_bass_kernel_spmd

    cos_q, sin_q, cos_k, sin_k = rope_tables()
    later = np.arange(T)[None, :] > np.arange(T)[:, None]
    arrays = {
        "x": L0_attn_x, "wq": L0_attn_Wq, "wkv": L0_attn_Wkv, "wo": L0_attn_Wo,
        "gate": np.transpose(L0_ffn_gate_w),
        "expert_w": np.transpose(L0_ffn_expert_w, (2, 0, 1)).reshape(DIM, EXPERTS * DIM),
        "expert_b": L0_ffn_expert_b, "c_t": np.transpose(L0_c), "wmod": L0_wmod,
        "cos_q": cos_q, "sin_q": sin_q, "cos_k": cos_k, "sin_k": sin_k,
        "ident": np.eye(T, dtype=np.float32),
        "mask": np.where(later, np.float32(MASKED), np.float32(0.0)),
    }
    arrays = {k: np.ascontiguousarray(v) for k, v in arrays.items()}
    nc = bacc.Bacc("TRN2", target_bir_lowering=False, num_devices=1)
    aps = [nc.dram_tensor(f"{k}_dram", v.shape, mybir.dt.from_np(v.dtype), kind="ExternalInput").ap()
           for k, v in arrays.items()]
    out = nc.dram_tensor("out_dram", (B, N, DIM), mybir.dt.float32, kind="ExternalOutput").ap()
    build(nc, *aps, out)
    r = run_bass_kernel_spmd(nc, [{f"{k}_dram": v for k, v in arrays.items()}], core_ids=[0])
    return r.results[0]["out_dram"]
```
